# Optimizing a Trainium2 kernel written in Bass

```python
import numpy as np
import jax
import jax.numpy as jnp

def _softmax(x, axis=-1):
    return jax.nn.softmax(x, axis=axis)

def _gelu(x):
    return jax.nn.gelu(x, approximate=True)

def _silu(x):
    return jax.nn.silu(x)

def _sigmoid(x):
    return jax.nn.sigmoid(x)

def _layernorm(x, axis=-1, eps=1e-05):
    m = jnp.mean(x, axis=axis, keepdims=True)
    v = jnp.var(x, axis=axis, keepdims=True)
    return (x - m) / jnp.sqrt(v + eps)

def _scatter_add(tgt, idx, src, axis=0):
    return tgt.at[idx].add(src)

def _segment_sum(src, seg, n):
    return jax.ops.segment_sum(src, seg, n)
kernel_name = 'mk_pixart_seq_d1_seqx_r2_67aa4b'

def setup_inputs(seed: int=0):
    np.random.seed(seed)
    _w = jnp.asarray

    def _rec_inputs():
        import jax
        import jax.numpy as jnp
        _rk = jax.random.key(seed)
        x = -0.0003929 + 0.9999 * jax.random.normal(jax.random.fold_in(_rk, 1), (16, 1024, 512), jnp.float32)
        _lenS = 1024 - jax.random.randint(jax.random.fold_in(_rk, 7), (16,), 0, max(1, 1024 // 4) + 1, jnp.int32)
        _lenS2 = 64 - jax.random.randint(jax.random.fold_in(_rk, 8), (16,), 0, max(1, 64 // 4) + 1, jnp.int32)
        _ctx_1024P = jax.random.normal(jax.random.fold_in(_rk, 11), (16, 16, 512), jnp.float32)
        _ctx_1024c = jax.random.dirichlet(jax.random.fold_in(_rk, 511), 0.3 * jnp.ones((16,), jnp.float32), (16, 64))
        _ctx_1024t = jnp.einsum('bsk,bkd->bsd', _ctx_1024c, _ctx_1024P)
        _ctx_1024t = _ctx_1024t * jax.lax.rsqrt(jnp.mean(jnp.square(_ctx_1024t)) + 1e-12) * 0.953939
        ctx_1024 = -1.39393e-06 + 0.999914 * (_ctx_1024t + 0.3 * jax.random.normal(jax.random.fold_in(_rk, 611), (16, 64, 512), jnp.float32))
        cond_1024 = -0.00920427 + 1.00102 * jax.random.normal(jax.random.fold_in(_rk, 12), (16, 512), jnp.float32)
        return (x, ctx_1024, cond_1024)
    x, ctx_1024, cond_1024 = _rec_inputs()

    def _L0_xcond_setup():
        import jax, jax.numpy as jnp
        import numpy as np
        EPS = 1e-05

        def _ada_ln(x, c, W_ss, b_ss):
            mu = jnp.mean(x, axis=-1, keepdims=True)
            var = jnp.mean((x - mu) ** 2, axis=-1, keepdims=True)
            h = (x - mu) / jnp.sqrt(var + EPS)
            ss = jax.nn.silu(c) @ W_ss + b_ss
            scale, bias = jnp.split(ss, 2, axis=-1)
            return (1.0 + scale)[:, None, :] * h + bias[:, None, :]
        key = jax.random.key(seed)
        ks = jax.random.split(key, 12)
        B, Lq, Lkv, H = (8, 1024, 256, 512)
        s = 0.02
        return {'x_q': jax.random.normal(ks[0], (B, Lq, H), jnp.float32), 'x_kv': jax.random.normal(ks[1], (B, Lkv, H), jnp.float32), 't_vec': jax.random.normal(ks[2], (B, H), jnp.float32), 'Wq': jax.random.normal(ks[3], (H, H), jnp.float32) * s, 'bq': jnp.zeros((H,), jnp.float32), 'Wkv': jax.random.normal(ks[4], (H, 2 * H), jnp.float32) * s, 'bkv': jnp.zeros((2 * H,), jnp.float32), 'Wp': jax.random.normal(ks[5], (H, H), jnp.float32) * s, 'bp': jnp.zeros((H,), jnp.float32), 'Wss_q': jax.random.normal(ks[6], (H, 2 * H), jnp.float32) * s, 'bss_q': jnp.zeros((2 * H,), jnp.float32), 'Wss_kv': jax.random.normal(ks[7], (H, 2 * H), jnp.float32) * s, 'bss_kv': jnp.zeros((2 * H,), jnp.float32)}
    _L0_xcond_all = _L0_xcond_setup()
    _L0_xcond_in = {k: v for k, v in _L0_xcond_all.items() if k in ('Wq', 'bq', 'Wkv', 'bkv', 'Wp', 'bp', 'Wss_q', 'bss_q', 'Wss_kv', 'bss_kv')}
    del _L0_xcond_all
    return {'x': x, 'ctx_1024': ctx_1024, 'cond_1024': cond_1024, 'L0_xcond_Wq': _L0_xcond_in['Wq'], 'L0_xcond_bq': _L0_xcond_in['bq'], 'L0_xcond_Wkv': _L0_xcond_in['Wkv'], 'L0_xcond_bkv': _L0_xcond_in['bkv'], 'L0_xcond_Wp': _L0_xcond_in['Wp'], 'L0_xcond_bp': _L0_xcond_in['bp'], 'L0_xcond_Wss_q': _L0_xcond_in['Wss_q'], 'L0_xcond_bss_q': _L0_xcond_in['bss_q'], 'L0_xcond_Wss_kv': _L0_xcond_in['Wss_kv'], 'L0_xcond_bss_kv': _L0_xcond_in['bss_kv']}

def reference(x, ctx_1024, cond_1024, L0_xcond_Wq, L0_xcond_bq, L0_xcond_Wkv, L0_xcond_bkv, L0_xcond_Wp, L0_xcond_bp, L0_xcond_Wss_q, L0_xcond_bss_q, L0_xcond_Wss_kv, L0_xcond_bss_kv):
    import jax
    import jax.numpy as jnp

    def _L0_xcond_ref(x_q, x_kv, t_vec, Wq, bq, Wkv, bkv, Wp, bp, Wss_q, bss_q, Wss_kv, bss_kv):
        import jax, jax.numpy as jnp
        import numpy as np
        EPS = 1e-05

        def _ada_ln(x, c, W_ss, b_ss):
            mu = jnp.mean(x, axis=-1, keepdims=True)
            var = jnp.mean((x - mu) ** 2, axis=-1, keepdims=True)
            h = (x - mu) / jnp.sqrt(var + EPS)
            ss = jax.nn.silu(c) @ W_ss + b_ss
            scale, bias = jnp.split(ss, 2, axis=-1)
            return (1.0 + scale)[:, None, :] * h + bias[:, None, :]
        B, Lq, H = x_q.shape
        Lkv = x_kv.shape[1]
        nh = 16
        dh = H // nh
        xq = _ada_ln(x_q, t_vec, Wss_q, bss_q)
        xkv = _ada_ln(x_kv, t_vec, Wss_kv, bss_kv)
        q = (xq @ Wq + bq).reshape(B, Lq, nh, dh)
        kv = (xkv @ Wkv + bkv).reshape(B, Lkv, 2, nh, dh)
        k = kv[:, :, 0]
        v = kv[:, :, 1]
        scores = jnp.einsum('bqhd,bkhd->bhqk', q, k) / jnp.sqrt(jnp.float32(dh))
        attn = jax.nn.softmax(scores, axis=-1)
        out = jnp.einsum('bhqk,bkhd->bqhd', attn, v).reshape(B, Lq, H)
        return x_q + (out @ Wp + bp)
    x = _L0_xcond_ref(x, ctx_1024, cond_1024, L0_xcond_Wq, L0_xcond_bq, L0_xcond_Wkv, L0_xcond_bkv, L0_xcond_Wp, L0_xcond_bp, L0_xcond_Wss_q, L0_xcond_bss_q, L0_xcond_Wss_kv, L0_xcond_bss_kv)
    return x

_drawn_inputs = setup_inputs


def setup_inputs(seed=0):
    import zlib

    import numpy as np

    out = dict(_drawn_inputs(seed))
    spreads = {'L0_xcond_bq': (0.0, 2.0),
     'L0_xcond_bkv': (0.0, 0.1),
     'L0_xcond_bp': (0.0, 0.1),
     'L0_xcond_bss_q': (0.0, 0.8),
     'L0_xcond_bss_kv': (0.0, 0.341)}
    factors = {'L0_xcond_Wq': 6.191, 'L0_xcond_Wss_q': 8.0}
    for name, (base, spread) in spreads.items():
        noise = np.random.default_rng([zlib.crc32(name.encode()), seed]).standard_normal(out[name].shape)
        drawn = base * np.exp(spread * noise) if base else spread * noise
        out[name] = jnp.asarray(drawn.astype(out[name].dtype))
    for name, factor in factors.items():
        out[name] = (out[name] * factor).astype(out[name].dtype)
    return out
```

```python
from contextlib import ExitStack

import concourse.bass as bass
from concourse import mybir

ALU = mybir.AluOpType
ACT = mybir.ActivationFunctionType
F32 = mybir.dt.float32
F32R = mybir.dt.float32r
F16 = mybir.dt.float16
U32 = mybir.dt.uint32
AX_X = mybir.AxisListType.X
ABSMAX = bass.bass_isa.ReduceOp.absmax

P = 128
EPS = 1e-5
EXPONENT_BITS = 0x7F800000
V_TOP = 2.0 ** 14


def adaln_cross_attention(nc, x, ctx_in, cond, Wq, bq, Wkv, bkv, Wp, bp, Wss_q, bss_q, Wss_kv, bss_kv, out):
    B, LQ, H = x.shape
    LKV = ctx_in.shape[1]
    DH = 32
    NH = H // DH
    KC = H // P
    PER = LQ // P
    TILE = 4
    UNITS = B * PER
    PAIRS = NH // 2
    HPG = P // DH
    VC = DH + 1
    CT = B * LKV // P
    HALF = NH // 2
    BH = 8
    assert P == 2 * LKV and H == 512 and PER == 2 * TILE and NH == KC * HPG

    with ExitStack() as ctx:
        def sb(name, shape, dt, stack=ctx):
            return stack.enter_context(nc.sbuf_tensor(name, shape, dt))

        def psum(name, shape):
            return ctx.enter_context(nc.psum_tensor(name, shape, F32))

        def sem(name):
            return ctx.enter_context(nc.semaphore(name))

        ps_s = psum("ps_s", [P, 2, 512])
        ps_t = psum("ps_t", [P, 2, 512])
        ps_q = psum("ps_q", [P, 512])
        ps_o = psum("ps_o", [P, 512])
        ps_v = psum("ps_v", [P, 2, 512])

        ident = sb("ident", [P, P], F32)
        wq = sb("wq", [P, KC, H], F32)
        wp_hi = sb("wp_hi", [P, KC, H], F32R)
        wp_lo = sb("wp_lo", [P, KC, H], F32R)
        w_tmp = sb("w_tmp", [P, KC, P], F32)
        w_hi = sb("w_hi", [P, KC, H], F32R)
        w_lo = sb("w_lo", [P, KC, H], F32R)
        k_all = sb("k_all", [P, B, KC, LKV], F32)
        cx = k_all[:].rearrange("p b k l -> p (b k l)").rearrange("p (t d) -> p t d", t=CT)
        kb_hi = sb("kb_hi", [P, KC, HPG, LKV], F32R)
        kb_lo = sb("kb_lo", [P, KC, HPG, LKV], F32R)
        v_all = sb("v_all", [P, 2, B, PAIRS, DH], F16)
        vb = sb("vb", [P, 2, PAIRS, 2, VC], F16)
        v_scale = sb("v_scale", [P, CT, NH], F32)
        v_inv = sb("v_inv", [P, CT, NH], F32)
        bp_row = sb("bp_row", [P, H], F32)
        ssq = sb("ssq", [P, 2, KC, B], F32)
        bqT = sb("bqT", [P, B, KC], F32)
        one_sc = sb("one_sc", [P, B, KC], F32)
        cur_bq = sb("cur_bq", [P, KC], F32)
        cur_sc = sb("cur_sc", [P, KC], F32)
        cur_vs = sb("cur_vs", [P, NH], F32)
        v_scale_b = sb("v_scale_b", [P, B, NH], F32)
        half_neg = sb("half_neg", [P, CT], F32)
        x_in = sb("x_in", [P, 4, H], F32)
        xr = sb("xr", [P, 4, H], F32)
        st = sb("st", [P, 6], F32)
        mv = sb("mv", [P, 2, 2], F32)
        nmv = sb("nmv", [P, 2, 2], F32)
        sign = sb("sign", [P, 2], F32)
        eps = sb("eps", [P, 1], F32)
        veps = sb("veps", [P, 2], F32)
        rstd = sb("rstd", [P, 2], F32)
        xh = sb("xh", [P, 2, H], F32)
        pr = sb("pr", [P, NH, LKV], F32)
        pt_hi = sb("pt_hi", [P, PAIRS, P], F16)
        pt_lo = sb("pt_lo", [P, PAIRS, P], F16)
        mx = sb("mx", [P, NH], F32)
        rden = sb("rden", [P, NH], F32)
        rscale = sb("rscale", [P, NH], F32)
        o = sb("o", [P, NH, DH], F32)
        oT_hi = sb("oT_hi", [P, KC, P], F32R)
        oT_lo = sb("oT_lo", [P, KC, P], F32R)


        BSSQ, BSSKV, BQ, BK, BV = 0, 2 * KC, 4 * KC, 5 * KC, 6 * KC
        row_slots = pr[:].rearrange("p h l -> p (h l)").rearrange("p (s n) -> p s n", s=2)
        o_slot = o[:].rearrange("p h d -> p (h d)")
        brow = o_slot[0:7 * KC, 0:P]
        c_row = row_slots[0:B, 0, :]
        turned = [row_slots[:, 0, :], row_slots[:, 1, :], o_slot]
        v16 = [t[:].rearrange("p g n -> p (g n)").rearrange("p (s n) -> p s n", s=2) for t in (pt_hi, pt_lo)]
        bv_cols = o_slot.rearrange("p (k n) -> p k n", k=KC)
        bias_t = sb("bias_t", [P, 7 * KC], F32)
        c_t = sb("c_t", [P, KC, B], F32)
        silu_t = sb("silu_t", [P, KC, B], F32)
        sig_t = sb("sig_t", [P, KC, B], F32)
        sh_q = sb("sh_q", [P, KC, B], F32)
        sc_kv = sb("sc_kv", [P, KC, B], F32)
        sh_kv = sb("sh_kv", [P, KC, B], F32)
        cst = sb("cst", [P, CT, 6], F32)
        cmv = sb("cmv", [P, CT, 2], F32)
        cveps = sb("cveps", [P, CT], F32)
        crstd = sb("crstd", [P, CT], F32)

        with ExitStack() as scratch:
            raw = sb("raw", [P, 8, KC * H], F32, scratch)
        xT_hi = sb("xT_hi", [P, 2, KC, 512], F32R)
        xT_lo = sb("xT_lo", [P, 2, KC, 512], F32R)
        q_hi = sb("q_hi", [P, 2, KC, 512], F32R)
        q_lo = sb("q_lo", [P, 2, KC, 512], F32R)
        cT_rest = sb("cT_rest", [P, 2, KC, 512], F32R)
        wk_raw = raw[:, 0, :].rearrange("p (k n) -> p k n", k=KC)
        wv_raw = raw[:, 2, :].rearrange("p (k n) -> p k n", k=KC)
        wss = [raw[:, 4 + 2 * a:6 + 2 * a, :].rearrange("p a n -> p (a n)").rearrange("p (k n) -> p k n", k=KC)
               for a in range(2)]
        mod_rows = [raw[0:B, 1 + 2 * a, 0:2 * H] for a in range(2)]
        wv_hi, wv_lo = xT_hi[:, 1], xT_lo[:, 1]
        wk_hi, wk_lo = wp_hi[:, :, :], wp_lo[:, :, :]
        cT_hi = [q_hi[:, 1], q_lo[:, 1]]
        cT_lo = [cT_rest[:, 0], cT_rest[:, 1]]
        wp_raw = xr[:, :, :]

        ld_small, ld_ctx, ld_ss, ld_ssq, ld_kv, ld_wq, ld_wp, ld_bp = (
            sem(n) for n in ("ld_small", "ld_ctx", "ld_ss", "ld_ssq", "ld_kv", "ld_wq", "ld_wp", "ld_bp"))
        id_zero, id_ready, zeros_ready, consts_ready, bd_ready = (
            sem(n) for n in ("id_zero", "id_ready", "zeros_ready", "consts_ready", "bd_ready"))
        small_turned, c_copied, c_exp, silu_step, mod_mm, mod_copied, mod_turned, mod_ready = (
            sem(n) for n in ("small_turned", "c_copied", "c_exp", "silu_step", "mod_mm", "mod_copied", "mod_turned",
                             "mod_ready"))
        bq_mm, bq_ready = sem("bq_mm"), sem("bq_ready")
        c_stats, c_mv, c_pool, cx_ready, cx_turned, c_mul, c_mod, cT_hi_done, cT_done = (
            sem(n) for n in ("c_stats", "c_mv", "c_pool", "cx_ready", "cx_turned", "c_mul", "c_mod", "cT_hi_done",
                             "cT_done"))
        wv_hi_done, wv_done, wk_hi_done, wk_done = (
            sem(n) for n in ("wv_hi_done", "wv_done", "wk_hi_done", "wk_done"))
        k_mm, k_ready, v_mm, v_copied, v_max, v_red, v_step, v_scaled, v_hi_done, v_lo_done, v_placed = (
            sem(n) for n in ("k_mm", "k_ready", "v_mm", "v_copied", "v_max", "v_red", "v_step", "v_scaled",
                             "v_hi_done", "v_lo_done", "v_placed"))
        wp_hi_done, wp_ready, bv_spread, bv_mm, bias_ready = (
            sem(n) for n in ("wp_hi_done", "wp_ready", "bv_spread", "bv_mm", "bias_ready"))

        x_loaded = [sem(f"x_loaded{i}") for i in range(4)]
        xr_loaded = [sem(f"xr_loaded{i}") for i in range(4)]
        stored = [sem(f"stored{i}") for i in range(4)]
        ln_bn, ln_mv, ln_step, xh_ready, xT_turned, xT_hi_done, xT_done = (
            sem(n) for n in ("ln_bn", "ln_mv", "ln_step", "xh_ready", "xT_turned", "xT_hi_done", "xT_done"))
        sc_staged, w_tmp_done, w_hi_done, w_done = (
            sem(n) for n in ("sc_staged", "w_tmp_done", "w_hi_done", "w_done"))
        bq_staged, q_mm, q_hi_done, q_done = (
            sem(n) for n in ("bq_staged", "q_mm", "q_hi_done", "q_done"))
        kb_hi_done, kb_done, vb_done, vs_staged = (
            sem(n) for n in ("kb_hi_done", "kb_done", "vb_done", "vs_staged"))
        s_mm, mx_done, sub_done, exp_done, p_turned, pt_hi_done, pt_done = (
            sem(n) for n in ("s_mm", "mx_done", "sub_done", "exp_done", "p_turned", "pt_hi_done", "pt_done"))
        pv_mm, rden_done, rscale_done, o_done, o_turned, oT_hi_done, oT_done = (
            sem(n) for n in ("pv_mm", "rden_done", "rscale_done", "o_done", "o_turned", "oT_hi_done", "oT_done"))
        vs_spread = sem("vs_spread")
        out_mm, xr_ready, y_ready = sem("out_mm"), sem("xr_ready"), sem("y_ready")

        x_units = x.rearrange("b (i p) d -> (b i) p d", p=P)
        out_units = out.rearrange("b (i p) d -> (b i) p d", p=P)

        def wait(eng, s, n):
            if not isinstance(n, int) or n > 0:
                eng.wait_ge(s, n)

        def unit(b, off):
            return PER * b + off

        def exists(b, off):
            return not isinstance(b, int) or 0 <= PER * b + off < UNITS

        def upto(b, off):
            n = PER * b + off + 1
            return min(max(n, 0), UNITS) if isinstance(b, int) else n

        def batch_exists(b):
            return not isinstance(b, int) or b < B

        def every_step(eng, step, prime=None):
            if prime:
                prime()
            for i in range(PER):
                step(0, i)
            with eng.Fori(1, B - 1) as b:
                for i in range(PER):
                    step(b, i)
            for i in range(PER):
                step(B - 1, i)
            for i in range(4):
                step(B, i)

        block = ctx.enter_context(nc.Block())

        @block.sync
        def _(sp):
            sp.dma_start(c_row, cond).then_inc(ld_small, 16)
            for at, v, n in ((BSSQ, bss_q, 2 * KC), (BSSKV, bss_kv, 2 * KC), (BQ, bq, KC), (BK, bkv, 2 * KC)):
                sp.dma_start(brow[at:at + n, :], v.rearrange("(r c) -> r c", c=P)).then_inc(ld_small, 16)
            for w, v, s in ((wss[0], Wss_kv, ld_ss), (None, ctx_in, ld_ctx), (wss[1], Wss_q, ld_ssq), (wq[:, :, :], Wq, ld_wq)):
                if w is None:
                    sp.dma_start(cx, v.rearrange("b l d -> (b l) d").rearrange("(t p) d -> p t d", p=P)).then_inc(s, 16)
                else:
                    sp.dma_start(w, v.rearrange("(k p) n -> p k n", p=P)).then_inc(s, 16)
            for w, at in ((wv_raw, H), (wk_raw, 0)):
                sp.dma_start(w, Wkv[:, at:at + H].rearrange("(k p) n -> p k n", p=P)).then_inc(ld_kv, 16)
            sp.dma_start(bp_row[:, :], bp.rearrange("(a n) -> a n", a=1).partition_broadcast(P)).then_inc(ld_bp, 16)

            def load_x(b, off):
                if not exists(b, off):
                    return
                wait(sp, xh_ready, unit(b, off - 3))
                sp.dma_start(x_in[:, off % 4, :], x_units[unit(b, off)]).then_inc(x_loaded[off % 4], 16)

            def load_xr(b, off):
                if not exists(b, off):
                    return
                wait(sp, stored[off % 4], 16 * (2 * b + off // 4))
                sp.dma_start(xr[:, off % 4, :], x_units[unit(b, off)]).then_inc(xr_loaded[off % 4], 16)

            def step(b, i):
                load_x(b, i + 12)
                load_xr(b, i)

            for f in range(4):
                load_x(0, f)
            sp.dma_start(wp_raw, Wp.rearrange("(k p) n -> p k n", p=P)).then_inc(ld_wp, 16)
            for f in range(4, 12):
                load_x(0, f)
            sp.wait_ge(wp_ready, 1)
            sp.wait_ge(bv_mm, 1)
            for i in range(PER):
                step(0, i)
            with sp.Fori(1, B - 2) as b:
                for i in range(PER):
                    step(b, i)
            for b in (B - 2, B - 1):
                for i in range(PER):
                    step(b, i)

        @block.gpsimd
        def _(pool):
            pool.memset(ident[:, :], 0.0).then_inc(id_zero, 1)
            pool.wait_ge(id_zero, 1)
            pool.affine_select(out=ident[:, :], in_=ident[:, :], compare_op=ALU.not_equal, fill=1.0,
                               base=0, pattern=[[-1, P]], channel_multiplier=1).then_inc(id_ready, 1)
            pool.memset(half_neg[:, :], -0.5).then_inc(consts_ready, 1)
            pool.memset(eps[:, :], EPS).then_inc(consts_ready, 1)
            pool.memset(sign[:, 0:1], -1.0).then_inc(consts_ready, 1)
            pool.memset(sign[:, 1:2], 1.0).then_inc(consts_ready, 1)
            pool.memset(kb_hi[:].bitcast(F32), 0.0).then_inc(bd_ready, 1)
            pool.memset(kb_lo[:].bitcast(F32), 0.0).then_inc(bd_ready, 1)
            pool.memset(vb[:, :, :, :, :], 0.0).then_inc(zeros_ready, 1)
            pool.wait_ge(zeros_ready, 1)
            for par in range(2):
                rows = slice(LKV * par, LKV * (par + 1))
                pool.memset(vb[rows, 0, :, par, DH:VC], 1.0).then_inc(bd_ready, 1)
                pool.wait_ge(bd_ready, 3 + par)

            pool.wait_ge(c_mv, CT)
            pool.tensor_scalar(cveps[:, :], cmv[:, :, 1], EPS, 1.0, ALU.add, ALU.mult).then_inc(c_pool, 1)
            pool.wait_ge(c_pool, 1)
            pool.wait_ge(consts_ready, 4)
            pool.tensor_tensor(crstd[:, :], cveps[:, :], half_neg[:, :], ALU.pow).then_inc(c_pool, 1)

            def context_lo(n):
                m, half = n // 2, n % 2
                pool.wait_ge(cT_hi_done, n + 1)
                pool.tensor_tensor(cT_lo[half][:, m, :], turned[n % 3], cT_hi[half][:, m, :].bitcast(F32),
                                   ALU.subtract).then_inc(cT_done, 1)

            def value_scale(t):
                pool.wait_ge(v_max, t + 1)
                pool.partition_all_reduce(v_scale[:, t, :], v_inv[:, t, :], P,
                                          bass.bass_isa.ReduceOp.max).then_inc(v_red, 1)
                pool.wait_ge(v_step, 3 * (t + 1))
                rows = row_slots[:, t % 2, :].rearrange("p (h d) -> p h d", d=DH)
                pool.tensor_tensor(rows, rows, v_inv[:, t, :].unsqueeze(2).to_broadcast([P, NH, DH]), ALU.mult)\
                    .then_inc(v_scaled, 1)

            def moments(b, off):
                if not exists(b, off):
                    return
                s = off % 2
                wait(pool, xh_ready, unit(b, off - 1))
                wait(pool, ln_mv, upto(b, off))
                pool.tensor_tensor(nmv[:, s, :], mv[:, s, :], sign[:, :], ALU.mult).then_inc(ln_step, 1)
                wait(pool, ln_step, 3 * unit(b, off) + 1)
                pool.tensor_tensor(veps[:, s:s + 1], nmv[:, s, 1:2], eps[:, :], ALU.add).then_inc(ln_step, 1)
                wait(pool, ln_step, 3 * unit(b, off) + 2)
                pool.tensor_tensor(rstd[:, s:s + 1], veps[:, s:s + 1], half_neg[:, 0:1], ALU.pow)\
                    .then_inc(ln_step, 1)

            def await_moments(b, off):
                if exists(b, off):
                    wait(pool, xT_turned, unit(b, off - 1))
                    wait(pool, ln_step, 3 * upto(b, off))

            def normalise(b, off):
                if exists(b, off):
                    s = off % 2
                    pool.tensor_scalar(xh[:, s, :], x_in[:, off % 4, :], nmv[:, s, 0:1], rstd[:, s:s + 1],
                                       ALU.add, ALU.mult).then_inc(xh_ready, 1)

            def residual(b, off):
                if exists(b, off):
                    s = off % 4
                    wait(pool, bias_ready, 1)
                    wait(pool, xr_loaded[s], 16 * (2 * b + off // 4 + 1))
                    pool.tensor_tensor(xr[:, s, :], xr[:, s, :], bp_row[:, :], ALU.add).then_inc(xr_ready, 1)

            def scaled_wq(b, m):
                if not batch_exists(b):
                    return
                if m == 0:
                    wait(pool, w_tmp_done, KC * b)
                    pool.tensor_copy(cur_sc[:, :], one_sc[:, b, :]).then_inc(sc_staged, 1)
                    wait(pool, sc_staged, b + 1)
                wait(pool, w_done, KC * b + m)
                pool.tensor_tensor(w_tmp[:, :, :], wq[:, :, m * P:(m + 1) * P],
                                   cur_sc[:, :].unsqueeze(2).to_broadcast([P, KC, P]), ALU.mult)\
                    .then_inc(w_tmp_done, 1)

            def keys_lo(b):
                if not batch_exists(b):
                    return
                for r in range(HPG):
                    rows = slice(DH * r, DH * (r + 1))
                    wait(pool, kb_hi_done, HPG * b + r + 1)
                    pool.tensor_tensor(kb_lo[rows, :, r, :], k_all[rows, b, :, :], kb_hi[rows, :, r, :].bitcast(F32),
                                       ALU.subtract).then_inc(kb_done, 1)
                    wait(pool, kb_done, HPG * b + r + 1)

            def step(b, i):
                moments(b, i + 8)
                await_moments(b, i + 8)
                residual(b, i - 3)
                normalise(b, i + 8)
                if 1 <= i <= 4:
                    scaled_wq(b + 1, i - 1)
                if i == 7:
                    keys_lo(b + 1)

            def prime():
                for n in range(2 * KC):
                    context_lo(n)
                pool.wait_ge(mod_ready, 4)
                pool.wait_ge(ld_wq, 16)
                for m in range(KC):
                    scaled_wq(0, m)

                def layernorm(f):
                    moments(0, f)
                    await_moments(0, f)
                    normalise(0, f)

                layernorm(0)
                layernorm(1)
                for t in range(CT):
                    value_scale(t)
                for n in range(6):
                    layernorm(n + 2)
                    if n == 4:
                        keys_lo(0)

            every_step(pool, step, prime)

        @block.scalar
        def _(act):
            act.wait_ge(c_copied, 1)
            act.activation(sig_t[:, :, :], c_t[:, :, :], ACT.Exp, scale=-1.0).then_inc(c_exp, 1)
            for side in range(2):
                act.wait_ge(mod_mm, side + 1)
                banks = (ps_s, ps_v)[side]
                act.copy(mod_rows[side].rearrange("b (a n) -> b a n", a=2), banks[0:B, :, :]).then_inc(mod_copied, 1)
            for n in range(2 * KC):
                act.wait_ge(c_mod, n + 1)
                act.copy(cT_hi[n % 2][:, n // 2, :], turned[n % 3]).then_inc(cT_hi_done, 1)

            def turned_x(b, off):
                if not exists(b, off):
                    return
                s = (off // 4) % 2
                cols = slice(P * (off % 4), P * (off % 4 + 1))
                wait(act, xT_turned, upto(b, off))
                if off % 4 == 0:
                    wait(act, q_mm, unit(b, off - 4))
                act.copy(xT_hi[:, s, :, cols], ps_t[:, 0, :].rearrange("p (k n) -> p k n", k=KC))\
                   .then_inc(xT_hi_done, 1)

            def turned_o(b, off):
                if not exists(b, off):
                    return
                wait(act, o_turned, upto(b, off))
                wait(act, out_mm, unit(b, off))
                act.copy(oT_hi[:, :, :], ps_t[:, 1, :].rearrange("p (k n) -> p k n", k=KC)).then_inc(oT_hi_done, 1)

            def keys_hi(b):
                if not batch_exists(b):
                    return
                wait(act, s_mm, 2 * PER * b)
                for r in range(HPG):
                    rows = slice(DH * r, DH * (r + 1))
                    act.copy(kb_hi[rows, :, r, :], k_all[rows, b, :, :]).then_inc(kb_hi_done, 1)

            def values(b):
                if not batch_exists(b):
                    return
                wait(act, pv_mm, 2 * PER * b)
                for part in range(2):
                    for par in range(2):
                        rows = slice(LKV * par, LKV * (par + 1))
                        act.copy(vb[rows, part, :, par, 0:DH], v_all[rows, part, b, :, :]).then_inc(vb_done, 1)

            def query_bias(b):
                if not batch_exists(b):
                    return
                wait(act, q_done, PER * b)
                act.copy(cur_bq[:, :], bqT[:, b, :]).then_inc(bq_staged, 1)
                wait(act, bq_staged, b + 1)

            def turned_p(b, off, h):
                if not exists(b, off):
                    return
                wait(act, p_turned, 2 * unit(b, off) + h + 1)
                if h == 0:
                    wait(act, pv_mm, 2 * unit(b, off))
                act.copy(pt_hi[:, 4 * h:4 * h + 4, :], ps_t[:, h, :].rearrange("p (g n) -> p g n", g=4))\
                   .then_inc(pt_hi_done, 1)

            def query(b, off):
                if not exists(b, off):
                    return
                s, m = (off // 4) % 2, off % 4
                wait(act, q_mm, upto(b, off))
                if m == 0:
                    wait(act, s_mm, 2 * unit(b, off - 4))
                act.activation(q_hi[:, s, m, :], ps_q[:, :], ACT.Identity, bias=cur_bq[:, m:m + 1])\
                   .then_inc(q_hi_done, 1)

            def scaled_wq_hi(b, m):
                if not batch_exists(b):
                    return
                wait(act, w_tmp_done, KC * b + m + 1)
                wait(act, q_mm, PER * (b - 1) + 4 + m + 1)
                act.copy(w_hi[:, :, m * P:(m + 1) * P], w_tmp[:, :, :]).then_inc(w_hi_done, 1)

            def step(b, i):
                turned_x(b, i + 7)
                turned_o(b, i - 3)
                if i == 1:
                    values(b)
                if i == 4:
                    query_bias(b + 1)
                if i == 7:
                    keys_hi(b + 1)
                turned_p(b, i - 1, 0)
                turned_p(b, i - 1, 1)
                query(b, i + 4)
                if exists(b, i):
                    wait(act, sub_done, 2 * upto(b, i))
                    act.activation(pr[:, :, :], pr[:, :, :], ACT.Exp).then_inc(exp_done, 1)
                if isinstance(b, int) and b == 0 and i == 0:
                    split_wp()
                if 1 <= i <= 4:
                    scaled_wq_hi(b + 1, i - 1)
                if exists(b, i - 4):
                    s = (i - 4) % 4
                    wait(act, y_ready, upto(b, i - 4))
                    act.dma_start(out_units[unit(b, i - 4)], xr[:, s, :]).then_inc(stored[s], 16)

            def split_wp():
                act.wait_ge(k_mm, 2 * KC)
                act.wait_ge(ld_wp, 16)
                act.copy(wp_hi[:, :, :], wp_raw).then_inc(wp_hi_done, 1)

            def prime():
                act.wait_ge(ld_kv, 32)
                act.copy(wv_hi, wv_raw).then_inc(wv_hi_done, 1)
                for m in range(KC):
                    scaled_wq_hi(0, m)
                act.copy(wk_hi, wk_raw).then_inc(wk_hi_done, 1)
                act.wait_ge(bq_ready, 1)
                query_bias(0)
                for t in range(CT + 1):
                    if t < CT:
                        act.wait_ge(v_mm, t + 1)
                        wait(act, v_lo_done, t - 1)
                        act.copy(row_slots[:, t % 2, :], ps_s[:, t % 2, :]).then_inc(v_copied, 1)
                    if t > 0:
                        act.wait_ge(v_scaled, t)
                        wait(act, v_placed, t - 2)
                        act.copy(v16[0][:, (t - 1) % 2, :], row_slots[:, (t - 1) % 2, :]).then_inc(v_hi_done, 1)
                act.wait_ge(wk_done, 1)
                for n in range(4):
                    turned_x(0, n)
                for n in range(4, 8):
                    query(0, n - 4)
                    if n == 4:
                        act.wait_ge(k_ready, KC)
                        act.wait_ge(bd_ready, 4)
                        keys_hi(0)
                    if n < 7:
                        turned_x(0, n)

            every_step(act, step, prime)
            for s in stored:
                act.wait_ge(s, 16 * (UNITS // 4))

        @block.vector
        def _(dve):
            dve.wait_ge(small_turned, 2)
            dve.tensor_copy(c_t[:, :, :], ps_t[:, 1, 0:KC * B].rearrange("p (k b) -> p k b", k=KC)).then_inc(c_copied, 1)
            dve.tensor_copy(bias_t[:, :], ps_t[:, 0, 0:7 * KC]).then_inc(c_copied, 1)
            dve.wait_ge(c_exp, 1)
            dve.tensor_scalar(sig_t[:, :, :], sig_t[:, :, :], 1.0, None, ALU.add).then_inc(silu_step, 1)
            dve.wait_ge(silu_step, 1)
            dve.reciprocal(sig_t[:, :, :], sig_t[:, :, :]).then_inc(silu_step, 1)
            dve.wait_ge(silu_step, 2)
            dve.wait_ge(c_copied, 2)
            dve.tensor_tensor(silu_t[:, :, :], sig_t[:, :, :], c_t[:, :, :], ALU.mult).then_inc(silu_step, 1)

            dve.wait_ge(ld_ctx, 16)
            for t in range(CT):
                dve.bn_stats(cst[:, t, :], cx[:, t, :]).then_inc(c_stats, 1)
            for t in range(CT):
                dve.wait_ge(c_stats, t + 1)
                dve.bn_aggr(cmv[:, t, :], cst[:, t, :]).then_inc(c_mv, 1)
            def modulation(side):
                at, outs = ((BSSKV, (sc_kv[:, :, :], sh_kv[:, :, :])),
                            (BSSQ, (one_sc[:].rearrange("p b k -> p k b"), sh_q[:, :, :])))[side]
                dve.wait_ge(mod_turned, side + 1)
                ps = ps_t[:, side, 0:2 * KC * B].rearrange("p (m b) -> p m b", b=B)
                for part, (o_ap, plus) in enumerate(zip(outs, (1.0, 0.0))):
                    bias = bias_t[:, at + KC * part:at + KC * (part + 1)].unsqueeze(2).to_broadcast([P, KC, B])
                    dve.scalar_tensor_tensor(out=o_ap, in0=ps[:, KC * part:KC * (part + 1), :], scalar=plus,
                                             in1=bias, op0=ALU.add, op1=ALU.add).then_inc(mod_ready, 1)

            modulation(0)
            dve.wait_ge(c_pool, 2)
            for t in range(CT):
                dve.tensor_scalar(cx[:, t, :], cx[:, t, :], cmv[:, t, 0:1], crstd[:, t:t + 1],
                                  ALU.subtract, ALU.mult).then_inc(cx_ready, 1)
            modulation(1)

            for n in range(2 * KC):
                k, half = n // 2, n % 2
                seg = turned[n % 3].rearrange("p (b l) -> p b l", b=BH)
                sc = sc_kv[:, k, BH * half:BH * (half + 1)].unsqueeze(2).to_broadcast([P, BH, LKV])
                sh = sh_kv[:, k, BH * half:BH * (half + 1)].unsqueeze(2).to_broadcast([P, BH, LKV])
                if n == 0:
                    dve.wait_ge(mod_ready, 2)
                dve.wait_ge(cx_turned, n + 1)
                wait(dve, cT_done, n - 2)
                dve.tensor_tensor(seg, ps_t[:, n % 2, :].rearrange("p (b l) -> p b l", b=BH), sc, ALU.mult)\
                   .then_inc(c_mul, 1)
                dve.wait_ge(c_mul, n + 1)
                dve.tensor_tensor(seg, seg, sh, ALU.add).then_inc(c_mod, 1)

            dve.wait_ge(bq_mm, 1)
            dve.tensor_tensor(bqT[:].rearrange("p b m -> p m b"),
                              ps_q[:, 0:KC * B].rearrange("p (m b) -> p m b", b=B),
                              bias_t[:, BQ:BQ + KC].unsqueeze(2).to_broadcast([P, KC, B]), ALU.add)\
               .then_inc(bq_ready, 1)

            def keys(n):
                half, m = n // KC, n % KC
                dve.wait_ge(k_mm, n + 1)
                dve.tensor_scalar(k_all[:, BH * half:BH * (half + 1), m, :],
                                  ps_v[:, n % 2, :].rearrange("p (b l) -> p b l", b=BH),
                                  bias_t[:, BK + m:BK + m + 1], DH ** -0.5, ALU.add, ALU.mult).then_inc(k_ready, 1)

            def value_max(t):
                dve.wait_ge(v_copied, t + 1)
                dve.tensor_reduce(v_inv[:, t, :], row_slots[:, t % 2, :].rearrange("p (h d) -> p h d", d=DH),
                                  AX_X, ALU.max, apply_absolute_value=True).then_inc(v_max, 1)

            def value_power(t):
                dve.wait_ge(v_red, t + 1)
                dve.tensor_scalar(v_scale[:, t, :], v_scale[:, t, :], 1e-30, 1.0 / V_TOP, ALU.max, ALU.mult)\
                   .then_inc(v_step, 1)
                dve.wait_ge(v_step, 3 * t + 1)
                dve.tensor_scalar(v_scale[:, t, :].bitcast(U32), v_scale[:, t, :].bitcast(U32), EXPONENT_BITS, None,
                                  ALU.bitwise_and).then_inc(v_step, 1)
                dve.wait_ge(v_step, 3 * t + 2)
                dve.reciprocal(v_inv[:, t, :], v_scale[:, t, :]).then_inc(v_step, 1)

            def value_place(t):
                s = t % 2
                dve.wait_ge(v_hi_done, t + 1)
                dve.tensor_tensor(v16[1][:, s, :], row_slots[:, s, :], v16[0][:, s, :], ALU.subtract)\
                   .then_inc(v_lo_done, 1)
                dve.wait_ge(v_lo_done, t + 1)
                for part in range(2):
                    for hb in range(2):
                        for par in range(2):
                            src = v16[part][LKV * hb:LKV * (hb + 1), s, :]\
                                .rearrange("p (g e d) -> p g e d", e=2, d=DH)[:, :, par, :]
                            last = dve.tensor_copy(v_all[LKV * par:LKV * (par + 1), part, 2 * t + hb, :, :], src)
                last.then_inc(v_placed, 1)

            def stats(b, off):
                if exists(b, off):
                    wait(dve, ln_mv, unit(b, off))
                    wait(dve, x_loaded[off % 4], 16 * (2 * b + off // 4 + 1))
                    dve.bn_stats(st[:, :], x_in[:, off % 4, :]).then_inc(ln_bn, 1)

            def await_stats(b, off):
                if exists(b, off):
                    wait(dve, xh_ready, unit(b, off - 1))
                    wait(dve, ln_bn, upto(b, off))

            def mean_var(b, off):
                if exists(b, off):
                    dve.bn_aggr(mv[:, off % 2, :], st[:, :]).then_inc(ln_mv, 1)

            def turned_x(b, off):
                if not exists(b, off):
                    return
                s = (off // 4) % 2
                cols = slice(P * (off % 4), P * (off % 4 + 1))
                wait(dve, xT_hi_done, upto(b, off))
                dve.tensor_tensor(xT_lo[:, s, :, cols], ps_t[:, 0, :].rearrange("p (k n) -> p k n", k=KC),
                                  xT_hi[:, s, :, cols].bitcast(F32), ALU.subtract).then_inc(xT_done, 1)

            def turned_o(b, off):
                if not exists(b, off):
                    return
                wait(dve, oT_hi_done, upto(b, off))
                dve.tensor_tensor(oT_lo[:, :, :], ps_t[:, 1, :].rearrange("p (k n) -> p k n", k=KC),
                                  oT_hi[:].bitcast(F32), ALU.subtract).then_inc(oT_done, 1)

            def normalise_o(b, off):
                if not exists(b, off):
                    return
                heads = ps_v[:, :, 0:HALF * VC].rearrange("p a (h c) -> p a h c", c=VC)
                for h in range(2):
                    wait(dve, pv_mm, 2 * unit(b, off) + h + 1)
                    dve.reciprocal(rden[:, HALF * h:HALF * (h + 1)], heads[:, h, :, DH]).then_inc(rden_done, 1)
                wait(dve, o_done, 2 * unit(b, off))
                wait(dve, rden_done, 2 * upto(b, off))
                dve.tensor_tensor(rscale[:, :], rden[:, :], cur_vs[:, :], ALU.mult).then_inc(rscale_done, 1)
                wait(dve, rscale_done, upto(b, off))
                wait(dve, o_turned, unit(b, off))
                for h in range(2):
                    hs = slice(HALF * h, HALF * (h + 1))
                    dve.tensor_tensor(o[:, hs, :], heads[:, h, :, 0:DH],
                                      rscale[:, hs].unsqueeze(2).to_broadcast([P, HALF, DH]), ALU.mult)\
                       .then_inc(o_done, 1)

            def result(b, off):
                if not exists(b, off):
                    return
                s = off % 4
                wait(dve, out_mm, upto(b, off))
                wait(dve, xr_ready, upto(b, off))
                dve.tensor_tensor(xr[:, s, :], ps_o[:, :], xr[:, s, :], ALU.add).then_inc(y_ready, 1)

            def softmax_shift(b, off):
                if not exists(b, off):
                    return
                for h in range(2):
                    wait(dve, s_mm, 2 * unit(b, off) + h + 1)
                    if h == 0:
                        wait(dve, sub_done, 2 * unit(b, off))
                    dve.tensor_reduce(mx[:, HALF * h:HALF * (h + 1)],
                                      ps_s[:, h, :].rearrange("p (h l) -> p h l", l=LKV), AX_X, ALU.max)\
                       .then_inc(mx_done, 1)
                wait(dve, p_turned, 2 * unit(b, off))
                for h in range(2):
                    hs = slice(HALF * h, HALF * (h + 1))
                    wait(dve, mx_done, 2 * unit(b, off) + h + 1)
                    dve.tensor_tensor(pr[:, hs, :], ps_s[:, h, :].rearrange("p (h l) -> p h l", l=LKV),
                                      mx[:, hs].unsqueeze(2).to_broadcast([P, HALF, LKV]), ALU.subtract)\
                       .then_inc(sub_done, 1)

            def turned_p(b, off, h):
                if not exists(b, off):
                    return
                wait(dve, pt_hi_done, 2 * unit(b, off) + h + 1)
                dve.tensor_tensor(pt_lo[:, 4 * h:4 * h + 4, :], ps_t[:, h, :].rearrange("p (g n) -> p g n", g=4),
                                  pt_hi[:, 4 * h:4 * h + 4, :], ALU.subtract).then_inc(pt_done, 1)

            def query(b, off):
                if not exists(b, off):
                    return
                s, m = (off // 4) % 2, off % 4
                wait(dve, q_hi_done, upto(b, off))
                dve.scalar_tensor_tensor(out=q_lo[:, s, m, :], in0=ps_q[:, :], scalar=cur_bq[:, m:m + 1],
                                         in1=q_hi[:, s, m, :].bitcast(F32), op0=ALU.add, op1=ALU.subtract)\
                   .then_inc(q_done, 1)

            def scaled_wq_lo(b, m):
                if not batch_exists(b):
                    return
                wait(dve, w_hi_done, KC * b + m + 1)
                cols = slice(P * m, P * (m + 1))
                dve.tensor_tensor(w_lo[:, :, cols], w_tmp[:, :, :], w_hi[:, :, cols].bitcast(F32), ALU.subtract)\
                   .then_inc(w_done, 1)

            def step(b, i):
                stats(b, i + 8)
                await_stats(b, i + 8)
                turned_x(b, i + 7)
                mean_var(b, i + 8)
                turned_o(b, i - 3)
                if i == 2 and batch_exists(b):
                    wait(dve, rscale_done, unit(b, 0))
                    dve.tensor_copy(cur_vs[:, :], v_scale_b[:, b, :]).then_inc(vs_staged, 1)
                    wait(dve, vs_staged, b + 1)
                normalise_o(b, i - 2)
                result(b, i - 4)
                softmax_shift(b, i)
                turned_p(b, i - 1, 0)
                turned_p(b, i - 1, 1)
                query(b, i + 4)
                if isinstance(b, int) and b == 0 and i == 0:
                    output_bias()
                    split_wp()
                if 1 <= i <= 4:
                    scaled_wq_lo(b + 1, i - 1)

            def split_wp():
                dve.wait_ge(bias_ready, 1)
                dve.wait_ge(wp_hi_done, 1)
                dve.tensor_tensor(wp_lo[:, :, :], wp_raw, wp_hi[:].bitcast(F32), ALU.subtract).then_inc(wp_ready, 1)

            def output_bias():
                dve.wait_ge(bv_mm, 1)
                dve.wait_ge(ld_bp, 16)
                dve.tensor_tensor(bp_row[:, :], ps_o[:, :], bp_row[:, :], ALU.add).then_inc(bias_ready, 1)

            def prime():
                def all_stats(f):
                    stats(0, f)
                    await_stats(0, f)
                    mean_var(0, f)

                dve.wait_ge(wv_hi_done, 1)
                dve.tensor_tensor(wv_lo, wv_raw, wv_hi.bitcast(F32), ALU.subtract).then_inc(wv_done, 1)
                for m in range(KC):
                    scaled_wq_lo(0, m)
                dve.wait_ge(wk_hi_done, 1)
                dve.tensor_tensor(wk_lo, wk_raw, wk_hi.bitcast(F32), ALU.subtract).then_inc(wk_done, 1)
                dve.tensor_copy(bv_cols, bias_t[:, BV:BV + KC].unsqueeze(2).to_broadcast([P, KC, P]))\
                   .then_inc(bv_spread, 1)
                all_stats(0)
                all_stats(1)
                for t in range(CT + 1):
                    if t < CT:
                        value_max(t)
                    if t > 0:
                        value_place(t - 1)
                    if t < CT:
                        value_power(t)
                dve.wait_ge(v_step, 3 * CT)
                dve.tensor_copy(v_scale_b[:].rearrange("p (t e) h -> p t e h", e=2),
                                v_scale[:].unsqueeze(2).to_broadcast([P, CT, 2, NH])).then_inc(vs_spread, 1)
                dve.wait_ge(vs_spread, 1)
                for n in range(8):
                    if n < 6:
                        all_stats(n + 2)
                    keys(n)
                    if n >= 4:
                        query(0, n - 4)
                    if n < 7:
                        turned_x(0, n)

            every_step(dve, step, prime)

        @block.tensor
        def _(pe):
            pe.wait_ge(id_ready, 1)
            pe.wait_ge(ld_small, 16 * 5)
            pe.transpose(ps_t[:, 0, 0:7 * KC], brow, ident[0:7 * KC, 0:7 * KC]).then_inc(small_turned, 1)
            for k in range(KC):
                last = pe.transpose(ps_t[:, 1, B * k:B * (k + 1)], c_row[:, P * k:P * (k + 1)], ident[0:B, 0:B])
            last.then_inc(small_turned, 1)

            pe.wait_ge(silu_step, 3)
            for side, landed in enumerate((ld_ss, ld_ssq)):
                banks = (ps_s, ps_v)[side]
                pe.wait_ge(landed, 16)
                for a in range(2):
                    for k in range(KC):
                        last = pe.matmul(banks[0:B, a, :], silu_t[:, k, :], wss[side][:, k, H * a:H * (a + 1)],
                                         start=(k == 0), stop=(k == KC - 1))
                last.then_inc(mod_mm, 1)
                pe.wait_ge(mod_copied, side + 1)
                for m in range(2 * KC):
                    last = pe.transpose(ps_t[:, side, B * m:B * (m + 1)], mod_rows[side][:, P * m:P * (m + 1)],
                                        ident[0:B, 0:B])
                last.then_inc(mod_turned, 1)

            pe.wait_ge(mod_ready, 4)
            for n in range(2 * KC):
                k, half = n // 2, n % 2
                wait(pe, c_mul, n - 1)
                for t in range(4):
                    pe.wait_ge(cx_ready, 4 * half + t + 1)
                    last = pe.transpose(ps_t[:, n % 2, P * t:P * (t + 1)], cx[:, 4 * half + t, P * k:P * (k + 1)],
                                        ident[:, :])
                last.then_inc(cx_turned, 1)

            pe.wait_ge(ld_wq, 16)
            for m in range(KC):
                for k in range(KC):
                    last = pe.matmul(ps_q[:, B * m:B * (m + 1)], wq[:, k, P * m:P * (m + 1)], sh_q[:, k, :],
                                     start=(k == 0), stop=(k == KC - 1))
            last.then_inc(bq_mm, 1)

            def split_product(dst, terms):
                last = None
                for n, (a, b) in enumerate((terms(p, k) for p in ((0, 0), (0, 1), (1, 0)) for k in range(KC))):
                    last = pe.matmul(dst, a, b, start=(n == 0), stop=(n == 3 * KC - 1))
                return last

            def value_rows(t):
                wait(pe, v_copied, t - 1)
                half, cols = t // 4, slice(P * (t % 4), P * (t % 4 + 1))
                split_product(ps_s[:, t % 2, :], lambda p, k: (
                    (cT_hi, cT_lo)[p[0]][half][:, k, cols], (wv_hi, wv_lo)[p[1]][:, k, :])).then_inc(v_mm, 1)

            def key_rows(n):
                half, m = n // KC, n % KC
                wait(pe, k_ready, n - 1)
                split_product(ps_v[:, n % 2, :], lambda p, k: (
                    (wk_hi, wk_lo)[p[0]][:, k, P * m:P * (m + 1)],
                    (cT_hi, cT_lo)[p[1]][half][:, k, :])).then_inc(k_mm, 1)

            def bias_product():
                pe.wait_ge(bv_spread, 1)
                pe.wait_ge(ld_wp, 16)
                for k in range(KC):
                    last = pe.matmul(ps_o[:, :], bv_cols[:, k, :], wp_raw[:, k, :], start=(k == 0), stop=(k == KC - 1))
                last.then_inc(bv_mm, 1)

            def turn_x(b, off):
                if not exists(b, off):
                    return
                wait(pe, xh_ready, upto(b, off))
                wait(pe, xT_done, unit(b, off))
                wait(pe, pt_done, 2 * unit(b, off - 9) + 1)
                for k in range(KC):
                    last = pe.transpose(ps_t[:, 0, P * k:P * (k + 1)], xh[:, off % 2, P * k:P * (k + 1)], ident[:, :])
                last.then_inc(xT_turned, 1)

            def project(b, off):
                if not exists(b, off):
                    return
                s, m = (off // 4) % 2, off % 4
                if m == 0:
                    wait(pe, xT_done, upto(b, off + 3))
                if off % PER < 4:
                    wait(pe, w_done, KC * (b + off // PER) + m + 1)
                wait(pe, q_done, unit(b, off))
                cols = slice(P * m, P * (m + 1))
                n = 0
                for w, xt in ((w_hi, xT_hi), (w_hi, xT_lo), (w_lo, xT_hi)):
                    for k in range(KC):
                        last = pe.matmul(ps_q[:, :], w[:, k, cols], xt[:, s, k, :], start=(n == 0),
                                         stop=(n == 3 * KC - 1))
                        n += 1
                last.then_inc(q_mm, 1)

            def score(b, off):
                if not exists(b, off):
                    return
                s = (off // 4) % 2
                cols = slice(P * (off % 4), P * (off % 4 + 1))
                if off % 4 == 0:
                    wait(pe, q_done, upto(b, off + 3))
                if off % PER == 0:
                    wait(pe, kb_done, HPG * (b + 1))
                for g in range(KC):
                    if g % 2 == 0:
                        wait(pe, sub_done, 2 * unit(b, off - 1) + g // 2 + 1)
                    dst = ps_s[:, g // 2, 256 * (g % 2):256 * (g % 2 + 1)]
                    for n, (qt, kt) in enumerate(((q_hi, kb_hi), (q_hi, kb_lo), (q_lo, kb_hi))):
                        last = pe.matmul(dst, qt[:, s, g, cols], kt[:, g, :, :].rearrange("p h l -> p (h l)"),
                                         start=(n == 0), stop=(n == 2))
                    if g % 2 == 1:
                        last.then_inc(s_mm, 1)

            def turn_p(b, off):
                if not exists(b, off):
                    return
                wait(pe, exp_done, upto(b, off))
                for h in range(2):
                    if h == 0:
                        wait(pe, xT_done, upto(b, off + 8))
                    else:
                        wait(pe, oT_done, unit(b, off - 1))
                    wait(pe, pt_done, 2 * unit(b, off - 1) + h + 1)
                    for g in range(4):
                        pair = 4 * h + g
                        last = pe.transpose(ps_t[:, h, P * g:P * (g + 1)],
                                            pr[:, 2 * pair:2 * pair + 2, :].rearrange("p h l -> p (h l)"),
                                            ident[:, :])
                    last.then_inc(p_turned, 1)

            def weigh(b, off):
                if not exists(b, off):
                    return
                if off % PER == 0:
                    wait(pe, vb_done, 4 * (b + off // PER + 1))
                wait(pe, o_done, 2 * unit(b, off))
                for h in range(2):
                    wait(pe, pt_done, 2 * unit(b, off) + h + 1)
                    for g in range(4):
                        pair = 4 * h + g
                        dst = ps_v[:, h, 2 * VC * g:2 * VC * (g + 1)]
                        for n, (pt, part) in enumerate(((pt_hi, 0), (pt_hi, 1), (pt_lo, 0))):
                            last = pe.matmul(dst, pt[:, pair, :],
                                             vb[:, part, pair, :, :].rearrange("p h c -> p (h c)"),
                                             start=(n == 0), stop=(n == 2))
                    last.then_inc(pv_mm, 1)

            def turn_o(b, off):
                if not exists(b, off):
                    return
                wait(pe, o_done, 2 * upto(b, off))
                wait(pe, oT_done, unit(b, off))
                wait(pe, pt_done, 2 * upto(b, off + 1))
                for k in range(KC):
                    last = pe.transpose(ps_t[:, 1, P * k:P * (k + 1)],
                                        o[:, HPG * k:HPG * (k + 1), :].rearrange("p h d -> p (h d)"), ident[:, :])
                last.then_inc(o_turned, 1)

            def project_out(b, off):
                if not exists(b, off):
                    return
                if isinstance(b, int) and b == 0:
                    wait(pe, wp_ready, 1)
                wait(pe, oT_done, upto(b, off))
                wait(pe, y_ready, unit(b, off))
                n = 0
                for ot, w in ((oT_hi, wp_hi), (oT_hi, wp_lo), (oT_lo, wp_hi)):
                    for k in range(KC):
                        last = pe.matmul(ps_o[:, :], ot[:, k, :], w[:, k, :], start=(n == 0), stop=(n == 3 * KC - 1))
                        n += 1
                last.then_inc(out_mm, 1)

            def step(b, i):
                score(b, i)
                turn_p(b, i - 1)
                project(b, i + 4)
                project_out(b, i - 3)
                turn_x(b, i + 8)
                turn_o(b, i - 2)
                weigh(b, i - 1)
                if isinstance(b, int) and b == 0 and i == 0:
                    bias_product()

            def prime():
                pe.wait_ge(cT_done, 2 * KC)
                pe.wait_ge(wv_done, 1)
                for t in range(CT):
                    value_rows(t)
                pe.wait_ge(wk_done, 1)
                pe.wait_ge(bq_ready, 1)
                for n in range(2 * KC):
                    key_rows(n)
                    if n >= 4:
                        project(0, n - 4)
                    turn_x(0, n)

            every_step(pe, step, prime)


_INS = ["x", "ctx_1024", "cond_1024", "L0_xcond_Wq", "L0_xcond_bq", "L0_xcond_Wkv", "L0_xcond_bkv", "L0_xcond_Wp",
        "L0_xcond_bp", "L0_xcond_Wss_q", "L0_xcond_bss_q", "L0_xcond_Wss_kv", "L0_xcond_bss_kv"]
_OUTS = [((16, 1024, 512), "float32")]


def kernel(**inputs):
    import numpy as _np
    import concourse.bacc as _bacc
    from concourse import mybir as _mybir
    from concourse.bass_utils import run_bass_kernel_spmd as _run

    nc = _bacc.Bacc("TRN2", target_bir_lowering=False, num_devices=1)
    arrays, args = {}, []
    for name in _INS:
        a = _np.ascontiguousarray(inputs[name])
        arrays[f"in_{name}_dram"] = a
        args.append(nc.dram_tensor(f"in_{name}_dram", a.shape, _mybir.dt.from_np(a.dtype), kind="ExternalInput").ap())
    for i, (shape, dtype) in enumerate(_OUTS):
        dt = _mybir.dt.from_np(_np.dtype(dtype))
        args.append(nc.dram_tensor(f"out_{i}_dram", shape, dt, kind="ExternalOutput").ap())
    adaln_cross_attention(nc, *args)
    r = _run(nc, [arrays], core_ids=[0])
    return r.results[0]["out_0_dram"]
```

```python
from contextlib import ExitStack

import concourse.bass as bass
from concourse import mybir

ALU = mybir.AluOpType
ACT = mybir.ActivationFunctionType
F32 = mybir.dt.float32
F32R = mybir.dt.float32r
F16 = mybir.dt.float16
U32 = mybir.dt.uint32
AX_X = mybir.AxisListType.X
ABSMAX = bass.bass_isa.ReduceOp.absmax

P = 128
EPS = 1e-5
EXPONENT_BITS = 0x7F800000
V_TOP = 2.0 ** 14


def adaln_cross_attention(nc, x, ctx_in, cond, Wq, bq, Wkv, bkv, Wp, bp, Wss_q, bss_q, Wss_kv, bss_kv, out):
    B, LQ, H = x.shape
    LKV = ctx_in.shape[1]
    DH = 32
    NH = H // DH
    KC = H // P
    PER = LQ // P
    TILE = 4
    UNITS = B * PER
    PAIRS = NH // 2
    HPG = P // DH
    VC = DH + 1
    CT = B * LKV // P
    HALF = NH // 2
    BH = 8
    assert P == 2 * LKV and H == 512 and PER == 2 * TILE and NH == KC * HPG

    with ExitStack() as ctx:
        def sb(name, shape, dt, stack=ctx):
            return stack.enter_context(nc.sbuf_tensor(name, shape, dt))

        def psum(name, shape):
            return ctx.enter_context(nc.psum_tensor(name, shape, F32))

        def sem(name):
            return ctx.enter_context(nc.semaphore(name))

        ps_s = psum("ps_s", [P, 2, 512])
        ps_t = psum("ps_t", [P, 2, 512])
        ps_q = psum("ps_q", [P, 512])
        ps_o = psum("ps_o", [P, 512])
        ps_v = psum("ps_v", [P, 2, 512])

        ident = sb("ident", [P, P], F32)
        wq = sb("wq", [P, KC, H], F32)
        wp_hi = sb("wp_hi", [P, KC, H], F32R)
        wp_lo = sb("wp_lo", [P, KC, H], F32R)
        w_tmp = sb("w_tmp", [P, KC, P], F32)
        w_hi = sb("w_hi", [P, KC, H], F32R)
        w_lo = sb("w_lo", [P, KC, H], F32R)
        k_all = sb("k_all", [P, B, KC, LKV], F32)
        cx = k_all[:].rearrange("p b k l -> p (b k l)").rearrange("p (t d) -> p t d", t=CT)
        kb_hi = sb("kb_hi", [P, KC, HPG, LKV], F32R)
        kb_lo = sb("kb_lo", [P, KC, HPG, LKV], F32R)
        v_all = sb("v_all", [P, 2, B, PAIRS, DH], F16)
        vb = sb("vb", [P, 2, PAIRS, 2, VC], F16)
        v_scale = sb("v_scale", [P, CT, NH], F32)
        v_inv = sb("v_inv", [P, CT, NH], F32)
        bp_row = sb("bp_row", [P, H], F32)
        ssq = sb("ssq", [P, 2, KC, B], F32)
        bqT = sb("bqT", [P, B, KC], F32)
        one_sc = sb("one_sc", [P, B, KC], F32)
        cur_bq = sb("cur_bq", [P, KC], F32)
        cur_sc = sb("cur_sc", [P, KC], F32)
        cur_vs = sb("cur_vs", [P, NH], F32)
        v_scale_b = sb("v_scale_b", [P, B, NH], F32)
        half_neg = sb("half_neg", [P, CT], F32)
        x_in = sb("x_in", [P, 4, H], F32)
        xr = sb("xr", [P, 4, H], F32)
        st = sb("st", [P, 6], F32)
        mv = sb("mv", [P, 2, 2], F32)
        nmv = sb("nmv", [P, 2, 2], F32)
        sign = sb("sign", [P, 2], F32)
        eps = sb("eps", [P, 1], F32)
        veps = sb("veps", [P, 2], F32)
        rstd = sb("rstd", [P, 2], F32)
        xh = sb("xh", [P, 2, H], F32)
        pr = sb("pr", [P, NH, LKV], F32)
        pt_hi = sb("pt_hi", [P, PAIRS, P], F16)
        pt_lo = sb("pt_lo", [P, PAIRS, P], F16)
        mx = sb("mx", [P, NH], F32)
        rden = sb("rden", [P, NH], F32)
        rscale = sb("rscale", [P, NH], F32)
        o = sb("o", [P, NH, DH], F32)
        oT_hi = sb("oT_hi", [P, KC, P], F32R)
        oT_lo = sb("oT_lo", [P, KC, P], F32R)


        BSSQ, BSSKV, BQ, BK, BV = 0, 2 * KC, 4 * KC, 5 * KC, 6 * KC
        row_slots = pr[:].rearrange("p h l -> p (h l)").rearrange("p (s n) -> p s n", s=2)
        o_slot = o[:].rearrange("p h d -> p (h d)")
        brow = o_slot[0:7 * KC, 0:P]
        c_row = row_slots[0:B, 0, :]
        v16 = [t[:].rearrange("p g n -> p (g n)").rearrange("p (s n) -> p s n", s=2) for t in (pt_hi, pt_lo)]
        bv_cols = o_slot.rearrange("p (k n) -> p k n", k=KC)
        bias_t = sb("bias_t", [P, 7 * KC], F32)
        c_t = sb("c_t", [P, KC, B], F32)
        silu_t = sb("silu_t", [P, KC, B], F32)
        sig_t = sb("sig_t", [P, KC, B], F32)
        sh_q = sb("sh_q", [P, KC, B], F32)
        sc_kv = sb("sc_kv", [P, KC, B], F32)
        sh_kv = sb("sh_kv", [P, KC, B], F32)
        cst = sb("cst", [P, CT, 6], F32)
        cmv = sb("cmv", [P, CT, 2], F32)
        cveps = sb("cveps", [P, CT], F32)
        crstd = sb("crstd", [P, CT], F32)

        with ExitStack() as scratch:
            raw = sb("raw", [P, 8, KC * H], F32, scratch)
        xT_hi = sb("xT_hi", [P, 2, KC, 512], F32R)
        xT_lo = sb("xT_lo", [P, 2, KC, 512], F32R)
        q_hi = sb("q_hi", [P, 2, KC, 512], F32R)
        q_lo = sb("q_lo", [P, 2, KC, 512], F32R)
        cT_rest = sb("cT_rest", [P, 2, KC, 512], F32R)
        wk_raw = raw[:, 0, :].rearrange("p (k n) -> p k n", k=KC)
        wv_raw = raw[:, 2, :].rearrange("p (k n) -> p k n", k=KC)
        wss = [raw[:, 4 + 2 * a:6 + 2 * a, :].rearrange("p a n -> p (a n)").rearrange("p (k n) -> p k n", k=KC)
               for a in range(2)]
        mod_rows = [raw[0:B, at, 0:2 * H] for at in (1, 6)]
        TURNED = 3
        turned = [raw[:, 4, H * a:H * (a + 1)] for a in range(TURNED)]
        wv_hi, wv_lo = xT_hi[:, 1], xT_lo[:, 1]
        wk_hi, wk_lo = wp_hi[:, :, :], wp_lo[:, :, :]
        cT_hi = [q_hi[:, 1], q_lo[:, 1]]
        cT_lo = [cT_rest[:, 0], cT_rest[:, 1]]
        wp_raw = xr[:, :, :]

        ld_small, ld_ctx, ld_wv, ld_wk, ld_wq, ld_wp, ld_bp = (
            sem(n) for n in ("ld_small", "ld_ctx", "ld_wv", "ld_wk", "ld_wq", "ld_wp", "ld_bp"))
        ld_ss = [sem(f"ld_ss{k}") for k in range(KC)]
        ld_ssq = [sem(f"ld_ssq{k}") for k in range(KC)]
        id_zero, id_ready, zeros_ready, consts_ready, bd_ready = (
            sem(n) for n in ("id_zero", "id_ready", "zeros_ready", "consts_ready", "bd_ready"))
        small_turned, c_copied, c_exp, silu_step, mod_mm, mod_copied, mod_turned, mod_ready = (
            sem(n) for n in ("small_turned", "c_copied", "c_exp", "silu_step", "mod_mm", "mod_copied", "mod_turned",
                             "mod_ready"))
        bq_mm, bq_ready = sem("bq_mm"), sem("bq_ready")
        c_stats, c_mv, c_pool, cx_ready, cx_turned, c_mul, c_mod, cT_hi_done, cT_done = (
            sem(n) for n in ("c_stats", "c_mv", "c_pool", "cx_ready", "cx_turned", "c_mul", "c_mod", "cT_hi_done",
                             "cT_done"))
        wv_hi_done, wv_done, wk_hi_done, wk_done = (
            sem(n) for n in ("wv_hi_done", "wv_done", "wk_hi_done", "wk_done"))
        k_mm, k_ready, v_mm, v_copied, v_max, v_red, v_step, v_scaled, v_hi_done, v_lo_done, v_hi_placed, v_placed = (
            sem(n) for n in ("k_mm", "k_ready", "v_mm", "v_copied", "v_max", "v_red", "v_step", "v_scaled",
                             "v_hi_done", "v_lo_done", "v_hi_placed", "v_placed"))
        wp_hi_done, wp_ready, bv_spread, bv_mm, bias_ready = (
            sem(n) for n in ("wp_hi_done", "wp_ready", "bv_spread", "bv_mm", "bias_ready"))

        x_loaded = [sem(f"x_loaded{i}") for i in range(4)]
        xr_loaded = [sem(f"xr_loaded{i}") for i in range(4)]
        stored = [sem(f"stored{i}") for i in range(4)]
        ln_bn, ln_mv, ln_step, xh_ready, xT_turned, xT_hi_done, xT_done = (
            sem(n) for n in ("ln_bn", "ln_mv", "ln_step", "xh_ready", "xT_turned", "xT_hi_done", "xT_done"))
        sc_staged, w_tmp_done, w_hi_done, w_done = (
            sem(n) for n in ("sc_staged", "w_tmp_done", "w_hi_done", "w_done"))
        bq_staged, q_mm, q_hi_done, q_done = (
            sem(n) for n in ("bq_staged", "q_mm", "q_hi_done", "q_done"))
        kb_hi_done, kb_done, vb_done, vs_staged = (
            sem(n) for n in ("kb_hi_done", "kb_done", "vb_done", "vs_staged"))
        s_mm, mx_done, sub_done, exp_done, p_turned, pt_hi_done, pt_done = (
            sem(n) for n in ("s_mm", "mx_done", "sub_done", "exp_done", "p_turned", "pt_hi_done", "pt_done"))
        pv_mm, rden_done, rscale_done, o_done, o_turned, oT_hi_done, oT_done = (
            sem(n) for n in ("pv_mm", "rden_done", "rscale_done", "o_done", "o_turned", "oT_hi_done", "oT_done"))
        vs_spread = sem("vs_spread")
        out_mm, xr_ready, y_ready = sem("out_mm"), sem("xr_ready"), sem("y_ready")

        x_units = x.rearrange("b (i p) d -> (b i) p d", p=P)
        out_units = out.rearrange("b (i p) d -> (b i) p d", p=P)

        def wait(eng, s, n):
            if not isinstance(n, int) or n > 0:
                eng.wait_ge(s, n)

        def unit(b, off):
            return PER * b + off

        def exists(b, off):
            return not isinstance(b, int) or 0 <= PER * b + off < UNITS

        def upto(b, off):
            n = PER * b + off + 1
            return min(max(n, 0), UNITS) if isinstance(b, int) else n

        def batch_exists(b):
            return not isinstance(b, int) or b < B

        def every_step(eng, step, prime=None):
            if prime:
                prime()
            for i in range(PER):
                step(0, i)
            with eng.Fori(1, B - 1) as b:
                for i in range(PER):
                    step(b, i)
            for i in range(PER):
                step(B - 1, i)
            for i in range(4):
                step(B, i)

        def place(copy, part, t):
            for hb in range(2):
                for par in range(2):
                    src = v16[part][LKV * hb:LKV * (hb + 1), t % 2, :]\
                        .rearrange("p (g e d) -> p g e d", e=2, d=DH)[:, :, par, :]
                    last = copy(v_all[LKV * par:LKV * (par + 1), part, 2 * t + hb, :, :], src)
            return last

        block = ctx.enter_context(nc.Block())

        @block.sync
        def _(sp):
            sp.dma_start(c_row, cond).then_inc(ld_small, 16)
            for at, v, n in ((BSSQ, bss_q, 2 * KC), (BSSKV, bss_kv, 2 * KC), (BQ, bq, KC), (BK, bkv, 2 * KC)):
                sp.dma_start(brow[at:at + n, :], v.rearrange("(r c) -> r c", c=P)).then_inc(ld_small, 16)
            for k in range(KC):
                sp.dma_start(wss[0][:, k, :], Wss_kv[P * k:P * (k + 1), :]).then_inc(ld_ss[k], 16)
            sp.dma_start(cx, ctx_in.rearrange("b l d -> (b l) d").rearrange("(t p) d -> p t d", p=P)).then_inc(ld_ctx, 16)
            for k in range(KC):
                sp.dma_start(wss[1][:, k, :], Wss_q[P * k:P * (k + 1), :]).then_inc(ld_ssq[k], 16)
            sp.dma_start(wv_raw, Wkv[:, H:2 * H].rearrange("(k p) n -> p k n", p=P)).then_inc(ld_wv, 16)
            sp.dma_start(wq[:, :, :], Wq.rearrange("(k p) n -> p k n", p=P)).then_inc(ld_wq, 16)
            sp.dma_start(wk_raw, Wkv[:, 0:H].rearrange("(k p) n -> p k n", p=P)).then_inc(ld_wk, 16)
            sp.dma_start(bp_row[:, :], bp.rearrange("(a n) -> a n", a=1).partition_broadcast(P)).then_inc(ld_bp, 16)

            def load_x(b, off):
                if not exists(b, off):
                    return
                wait(sp, xh_ready, unit(b, off - 3))
                sp.dma_start(x_in[:, off % 4, :], x_units[unit(b, off)]).then_inc(x_loaded[off % 4], 16)

            def load_xr(b, off):
                if not exists(b, off):
                    return
                wait(sp, stored[off % 4], 16 * (2 * b + off // 4))
                sp.dma_start(xr[:, off % 4, :], x_units[unit(b, off)]).then_inc(xr_loaded[off % 4], 16)

            def step(b, i):
                load_x(b, i + 12)
                load_xr(b, i)

            for f in range(4):
                load_x(0, f)
            sp.dma_start(wp_raw, Wp.rearrange("(k p) n -> p k n", p=P)).then_inc(ld_wp, 16)
            for f in range(4, 12):
                load_x(0, f)
            sp.wait_ge(wp_ready, 2)
            sp.wait_ge(bv_mm, 1)
            for i in range(PER):
                step(0, i)
            with sp.Fori(1, B - 2) as b:
                for i in range(PER):
                    step(b, i)
            for b in (B - 2, B - 1):
                for i in range(PER):
                    step(b, i)

        @block.gpsimd
        def _(pool):
            pool.memset(ident[:, :], 0.0).then_inc(id_zero, 1)
            pool.wait_ge(id_zero, 1)
            pool.affine_select(out=ident[:, :], in_=ident[:, :], compare_op=ALU.not_equal, fill=1.0,
                               base=0, pattern=[[-1, P]], channel_multiplier=1).then_inc(id_ready, 1)
            pool.memset(half_neg[:, :], -0.5).then_inc(consts_ready, 1)
            pool.memset(eps[:, :], EPS).then_inc(consts_ready, 1)
            pool.memset(sign[:, 0:1], -1.0).then_inc(consts_ready, 1)
            pool.memset(sign[:, 1:2], 1.0).then_inc(consts_ready, 1)
            pool.memset(kb_hi[:].bitcast(F32), 0.0).then_inc(bd_ready, 1)
            pool.memset(kb_lo[:].bitcast(F32), 0.0).then_inc(bd_ready, 1)
            pool.memset(vb[:, :, :, :, :], 0.0).then_inc(zeros_ready, 1)
            pool.wait_ge(zeros_ready, 1)
            for par in range(2):
                rows = slice(LKV * par, LKV * (par + 1))
                pool.memset(vb[rows, 0, :, par, DH:VC], 1.0).then_inc(bd_ready, 1)
                pool.wait_ge(bd_ready, 3 + par)

            pool.wait_ge(c_mv, CT)
            pool.tensor_scalar(cveps[:, :], cmv[:, :, 1], EPS, 1.0, ALU.add, ALU.mult).then_inc(c_pool, 1)
            pool.wait_ge(c_pool, 1)
            pool.wait_ge(consts_ready, 4)
            pool.tensor_tensor(crstd[:, :], cveps[:, :], half_neg[:, :], ALU.pow).then_inc(c_pool, 1)

            def context_lo(n):
                half, m = n // KC, n % KC
                pool.wait_ge(cT_hi_done, n + 1)
                pool.tensor_tensor(cT_lo[half][:, m, :], turned[n % TURNED], cT_hi[half][:, m, :].bitcast(F32),
                                   ALU.subtract).then_inc(cT_done, 1)

            def value_scale(t):
                pool.wait_ge(v_max, t + 1)
                pool.partition_all_reduce(v_scale[:, t, :], v_inv[:, t, :], P,
                                          bass.bass_isa.ReduceOp.max).then_inc(v_red, 1)
                pool.wait_ge(v_step, 3 * (t + 1))
                rows = row_slots[:, t % 2, :].rearrange("p (h d) -> p h d", d=DH)
                pool.tensor_tensor(rows, rows, v_inv[:, t, :].unsqueeze(2).to_broadcast([P, NH, DH]), ALU.mult)\
                    .then_inc(v_scaled, 1)

            def moments(b, off):
                if not exists(b, off):
                    return
                s = off % 2
                wait(pool, xh_ready, unit(b, off - 1))
                wait(pool, ln_mv, upto(b, off))
                pool.tensor_tensor(nmv[:, s, :], mv[:, s, :], sign[:, :], ALU.mult).then_inc(ln_step, 1)
                wait(pool, ln_step, 3 * unit(b, off) + 1)
                pool.tensor_tensor(veps[:, s:s + 1], nmv[:, s, 1:2], eps[:, :], ALU.add).then_inc(ln_step, 1)
                wait(pool, ln_step, 3 * unit(b, off) + 2)
                pool.tensor_tensor(rstd[:, s:s + 1], veps[:, s:s + 1], half_neg[:, 0:1], ALU.pow)\
                    .then_inc(ln_step, 1)

            def await_moments(b, off):
                if exists(b, off):
                    wait(pool, xT_turned, unit(b, off - 1))
                    wait(pool, ln_step, 3 * upto(b, off))

            def normalise(b, off):
                if exists(b, off):
                    s = off % 2
                    pool.tensor_scalar(xh[:, s, :], x_in[:, off % 4, :], nmv[:, s, 0:1], rstd[:, s:s + 1],
                                       ALU.add, ALU.mult).then_inc(xh_ready, 1)

            def residual(b, off):
                if exists(b, off):
                    s = off % 4
                    wait(pool, bias_ready, 1)
                    wait(pool, xr_loaded[s], 16 * (2 * b + off // 4 + 1))
                    pool.tensor_tensor(xr[:, s, :], xr[:, s, :], bp_row[:, :], ALU.add).then_inc(xr_ready, 1)

            def scaled_wq(b, m):
                if not batch_exists(b):
                    return
                if m == 0:
                    wait(pool, w_tmp_done, KC * b)
                    pool.tensor_copy(cur_sc[:, :], one_sc[:, b, :]).then_inc(sc_staged, 1)
                    wait(pool, sc_staged, b + 1)
                wait(pool, w_done, KC * b + m)
                pool.tensor_tensor(w_tmp[:, :, :], wq[:, :, m * P:(m + 1) * P],
                                   cur_sc[:, :].unsqueeze(2).to_broadcast([P, KC, P]), ALU.mult)\
                    .then_inc(w_tmp_done, 1)

            def keys_lo(b):
                if not batch_exists(b):
                    return
                for r in range(HPG):
                    rows = slice(DH * r, DH * (r + 1))
                    wait(pool, kb_hi_done, HPG * b + r + 1)
                    pool.tensor_tensor(kb_lo[rows, :, r, :], k_all[rows, b, :, :], kb_hi[rows, :, r, :].bitcast(F32),
                                       ALU.subtract).then_inc(kb_done, 1)
                    wait(pool, kb_done, HPG * b + r + 1)

            def step(b, i):
                moments(b, i + 8)
                await_moments(b, i + 8)
                residual(b, i - 3)
                normalise(b, i + 8)
                if 1 <= i <= 4:
                    scaled_wq(b + 1, i - 1)
                if i == 7:
                    keys_lo(b + 1)

            def prime():
                def layernorm(f):
                    moments(0, f)
                    await_moments(0, f)
                    normalise(0, f)

                for n in range(2 * KC):
                    context_lo(n)
                    if n == KC:
                        pool.wait_ge(mod_ready, 4)
                        pool.wait_ge(ld_wq, 16)
                    if n >= KC:
                        scaled_wq(0, n - KC)
                    if n >= 2 + KC:
                        layernorm(n - 2 - KC)
                for t in range(CT):
                    value_scale(t)
                    if 1 <= t <= 4:
                        layernorm(t + 1)
                    if t == 5:
                        keys_lo(0)
                layernorm(6)
                layernorm(7)

            every_step(pool, step, prime)

        @block.scalar
        def _(act):
            act.wait_ge(c_copied, 1)
            act.activation(sig_t[:, :, :], c_t[:, :, :], ACT.Exp, scale=-1.0).then_inc(c_exp, 1)
            for side in range(2):
                if side == 1:
                    act.wait_ge(ld_wv, 16)
                    act.wait_ge(mod_turned, 1)
                    act.copy(wv_hi, wv_raw).then_inc(wv_hi_done, 1)
                act.wait_ge(mod_mm, side + 1)
                banks = (ps_s, ps_v)[side]
                act.copy(mod_rows[side].rearrange("b (a n) -> b a n", a=2), banks[0:B, :, :]).then_inc(mod_copied, 1)
            def turned_x(b, off):
                if not exists(b, off):
                    return
                s = (off // 4) % 2
                cols = slice(P * (off % 4), P * (off % 4 + 1))
                wait(act, xT_turned, upto(b, off))
                if off % 4 == 0:
                    wait(act, q_mm, unit(b, off - 4))
                act.copy(xT_hi[:, s, :, cols], ps_t[:, 0, :].rearrange("p (k n) -> p k n", k=KC))\
                   .then_inc(xT_hi_done, 1)

            def turned_o(b, off):
                if not exists(b, off):
                    return
                wait(act, o_turned, upto(b, off))
                wait(act, out_mm, unit(b, off))
                act.copy(oT_hi[:, :, :], ps_t[:, 1, :].rearrange("p (k n) -> p k n", k=KC)).then_inc(oT_hi_done, 1)

            def keys_hi(b):
                if not batch_exists(b):
                    return
                wait(act, s_mm, 2 * PER * b)
                for r in range(HPG):
                    rows = slice(DH * r, DH * (r + 1))
                    act.copy(kb_hi[rows, :, r, :], k_all[rows, b, :, :]).then_inc(kb_hi_done, 1)

            def values(b):
                if not batch_exists(b):
                    return
                wait(act, pv_mm, 2 * PER * b)
                for part in range(2):
                    for par in range(2):
                        rows = slice(LKV * par, LKV * (par + 1))
                        act.copy(vb[rows, part, :, par, 0:DH], v_all[rows, part, b, :, :]).then_inc(vb_done, 1)

            def query_bias(b):
                if not batch_exists(b):
                    return
                wait(act, q_done, PER * b)
                act.copy(cur_bq[:, :], bqT[:, b, :]).then_inc(bq_staged, 1)
                wait(act, bq_staged, b + 1)

            def turned_p(b, off, h):
                if not exists(b, off):
                    return
                wait(act, p_turned, 2 * unit(b, off) + h + 1)
                if h == 0:
                    wait(act, pv_mm, 2 * unit(b, off))
                act.copy(pt_hi[:, 4 * h:4 * h + 4, :], ps_t[:, h, :].rearrange("p (g n) -> p g n", g=4))\
                   .then_inc(pt_hi_done, 1)

            def query(b, off):
                if not exists(b, off):
                    return
                s, m = (off // 4) % 2, off % 4
                wait(act, q_mm, upto(b, off))
                if m == 0:
                    wait(act, s_mm, 2 * unit(b, off - 4))
                act.activation(q_hi[:, s, m, :], ps_q[:, :], ACT.Identity, bias=cur_bq[:, m:m + 1])\
                   .then_inc(q_hi_done, 1)

            def scaled_wq_hi(b, m):
                if not batch_exists(b):
                    return
                wait(act, w_tmp_done, KC * b + m + 1)
                wait(act, q_mm, PER * (b - 1) + 4 + m + 1)
                act.copy(w_hi[:, :, m * P:(m + 1) * P], w_tmp[:, :, :]).then_inc(w_hi_done, 1)

            def step(b, i):
                turned_x(b, i + 7)
                turned_o(b, i - 3)
                if i == 1:
                    values(b)
                if i == 4:
                    query_bias(b + 1)
                if i == 7:
                    keys_hi(b + 1)
                turned_p(b, i - 1, 0)
                turned_p(b, i - 1, 1)
                query(b, i + 4)
                if exists(b, i):
                    wait(act, sub_done, 2 * upto(b, i))
                    act.activation(pr[:, :, :], pr[:, :, :], ACT.Exp).then_inc(exp_done, 1)
                if isinstance(b, int) and b == 0 and i < 2:
                    wp_high(i)
                if 1 <= i <= 4:
                    scaled_wq_hi(b + 1, i - 1)
                if exists(b, i - 4):
                    s = (i - 4) % 4
                    wait(act, y_ready, upto(b, i - 4))
                    act.dma_start(out_units[unit(b, i - 4)], xr[:, s, :]).then_inc(stored[s], 16)

            def wp_high(part):
                act.wait_ge(k_mm, 2 * KC)
                act.wait_ge(ld_wp, 16)
                ks = slice(KC // 2 * part, KC // 2 * (part + 1))
                act.copy(wp_hi[:, ks, :], wp_raw[:, ks, :]).then_inc(wp_hi_done, 1)

            def prime():
                for n in range(2 * KC):
                    act.wait_ge(c_mod, n + 1)
                    act.copy(cT_hi[n // KC][:, n % KC, :], turned[n % TURNED]).then_inc(cT_hi_done, 1)
                    if n > KC:
                        scaled_wq_hi(0, n - KC - 1)
                    if n == KC - 1:
                        act.wait_ge(ld_wk, 16)
                        act.copy(wk_hi, wk_raw).then_inc(wk_hi_done, 1)
                scaled_wq_hi(0, KC - 1)
                act.wait_ge(wk_done, 1)
                for t in range(CT + 1):
                    if t < CT:
                        act.wait_ge(v_mm, t + 1)
                        wait(act, v_lo_done, t - 1)
                        act.copy(row_slots[:, t % 2, :], ps_s[:, t % 2, :]).then_inc(v_copied, 1)
                    if t == CT - 1:
                        turned_x(0, KC)
                    if t > 0:
                        value_hi(t - 1)
                    if 1 <= t <= KC:
                        turned_x(0, t - 1)
                    if t == KC + 1:
                        act.wait_ge(bq_ready, 1)
                        query_bias(0)
                        act.wait_ge(k_ready, KC)
                        act.wait_ge(bd_ready, 4)
                        keys_hi(0)
                    if t == CT - 1:
                        turned_x(0, KC + 1)
                    if t == CT:
                        turned_x(0, KC + 2)
                    if t > KC:
                        query(0, t - KC - 1)

            def value_hi(t):
                act.wait_ge(v_scaled, t + 1)
                wait(act, v_placed, t - 1)
                wait(act, v_hi_placed, t - 1)
                act.copy(v16[0][:, t % 2, :], row_slots[:, t % 2, :]).then_inc(v_hi_done, 1)
                act.wait_ge(v_hi_done, t + 1)
                place(act.copy, 0, t).then_inc(v_hi_placed, 1)

            every_step(act, step, prime)
            for s in stored:
                act.wait_ge(s, 16 * (UNITS // 4))

        @block.vector
        def _(dve):
            dve.wait_ge(small_turned, 2)
            dve.tensor_copy(c_t[:, :, :], ps_t[:, 1, 0:KC * B].rearrange("p (k b) -> p k b", k=KC)).then_inc(c_copied, 1)
            dve.tensor_copy(bias_t[:, :], ps_t[:, 0, 0:7 * KC]).then_inc(c_copied, 1)
            dve.wait_ge(c_exp, 1)
            dve.tensor_scalar(sig_t[:, :, :], sig_t[:, :, :], 1.0, None, ALU.add).then_inc(silu_step, 1)
            dve.wait_ge(silu_step, 1)
            dve.reciprocal(sig_t[:, :, :], sig_t[:, :, :]).then_inc(silu_step, 1)
            dve.wait_ge(silu_step, 2)
            dve.wait_ge(c_copied, 2)
            dve.tensor_tensor(silu_t[:, :, :], sig_t[:, :, :], c_t[:, :, :], ALU.mult).then_inc(silu_step, 1)

            dve.wait_ge(ld_ctx, 16)
            for t in range(CT):
                dve.bn_stats(cst[:, t, :], cx[:, t, :]).then_inc(c_stats, 1)
            for t in range(CT):
                dve.wait_ge(c_stats, t + 1)
                dve.bn_aggr(cmv[:, t, :], cst[:, t, :]).then_inc(c_mv, 1)
            def modulation(side):
                at, outs = ((BSSKV, (sc_kv[:, :, :], sh_kv[:, :, :])),
                            (BSSQ, (one_sc[:].rearrange("p b k -> p k b"), sh_q[:, :, :])))[side]
                dve.wait_ge(mod_turned, side + 1)
                ps = ps_t[:, side, 0:2 * KC * B].rearrange("p (m b) -> p m b", b=B)
                for part, (o_ap, plus) in enumerate(zip(outs, (1.0, 0.0))):
                    bias = bias_t[:, at + KC * part:at + KC * (part + 1)].unsqueeze(2).to_broadcast([P, KC, B])
                    dve.scalar_tensor_tensor(out=o_ap, in0=ps[:, KC * part:KC * (part + 1), :], scalar=plus,
                                             in1=bias, op0=ALU.add, op1=ALU.add).then_inc(mod_ready, 1)

            modulation(0)
            dve.wait_ge(c_pool, 2)
            for t in range(CT):
                dve.tensor_scalar(cx[:, t, :], cx[:, t, :], cmv[:, t, 0:1], crstd[:, t:t + 1],
                                  ALU.subtract, ALU.mult).then_inc(cx_ready, 1)
            dve.wait_ge(wv_hi_done, 1)
            dve.tensor_tensor(wv_lo, wv_raw, wv_hi.bitcast(F32), ALU.subtract).then_inc(wv_done, 1)

            def keys(n):
                half, m = n // KC, n % KC
                dve.wait_ge(k_mm, n + 1)
                dve.tensor_scalar(k_all[:, BH * half:BH * (half + 1), m, :],
                                  ps_v[:, n % 2, :].rearrange("p (b l) -> p b l", b=BH),
                                  bias_t[:, BK + m:BK + m + 1], DH ** -0.5, ALU.add, ALU.mult).then_inc(k_ready, 1)

            def value_max(t):
                dve.wait_ge(v_copied, t + 1)
                dve.tensor_reduce(v_inv[:, t, :], row_slots[:, t % 2, :].rearrange("p (h d) -> p h d", d=DH),
                                  AX_X, ALU.max, apply_absolute_value=True).then_inc(v_max, 1)

            def value_power(t):
                dve.wait_ge(v_red, t + 1)
                dve.tensor_scalar(v_scale[:, t, :], v_scale[:, t, :], 1e-30, 1.0 / V_TOP, ALU.max, ALU.mult)\
                   .then_inc(v_step, 1)
                dve.wait_ge(v_step, 3 * t + 1)
                dve.tensor_scalar(v_scale[:, t, :].bitcast(U32), v_scale[:, t, :].bitcast(U32), EXPONENT_BITS, None,
                                  ALU.bitwise_and).then_inc(v_step, 1)
                dve.wait_ge(v_step, 3 * t + 2)
                dve.reciprocal(v_inv[:, t, :], v_scale[:, t, :]).then_inc(v_step, 1)

            def value_place(t):
                s = t % 2
                dve.wait_ge(v_hi_done, t + 1)
                dve.tensor_tensor(v16[1][:, s, :], row_slots[:, s, :], v16[0][:, s, :], ALU.subtract)\
                   .then_inc(v_lo_done, 1)
                dve.wait_ge(v_lo_done, t + 1)
                place(dve.tensor_copy, 1, t).then_inc(v_placed, 1)

            def stats(b, off):
                if exists(b, off):
                    wait(dve, ln_mv, unit(b, off))
                    wait(dve, x_loaded[off % 4], 16 * (2 * b + off // 4 + 1))
                    dve.bn_stats(st[:, :], x_in[:, off % 4, :]).then_inc(ln_bn, 1)

            def await_stats(b, off):
                if exists(b, off):
                    wait(dve, xh_ready, unit(b, off - 1))
                    wait(dve, ln_bn, upto(b, off))

            def mean_var(b, off):
                if exists(b, off):
                    dve.bn_aggr(mv[:, off % 2, :], st[:, :]).then_inc(ln_mv, 1)

            def turned_x(b, off):
                if not exists(b, off):
                    return
                s = (off // 4) % 2
                cols = slice(P * (off % 4), P * (off % 4 + 1))
                wait(dve, xT_hi_done, upto(b, off))
                dve.tensor_tensor(xT_lo[:, s, :, cols], ps_t[:, 0, :].rearrange("p (k n) -> p k n", k=KC),
                                  xT_hi[:, s, :, cols].bitcast(F32), ALU.subtract).then_inc(xT_done, 1)

            def turned_o(b, off):
                if not exists(b, off):
                    return
                wait(dve, oT_hi_done, upto(b, off))
                dve.tensor_tensor(oT_lo[:, :, :], ps_t[:, 1, :].rearrange("p (k n) -> p k n", k=KC),
                                  oT_hi[:].bitcast(F32), ALU.subtract).then_inc(oT_done, 1)

            def normalise_o(b, off):
                if not exists(b, off):
                    return
                heads = ps_v[:, :, 0:HALF * VC].rearrange("p a (h c) -> p a h c", c=VC)
                for h in range(2):
                    wait(dve, pv_mm, 2 * unit(b, off) + h + 1)
                    dve.reciprocal(rden[:, HALF * h:HALF * (h + 1)], heads[:, h, :, DH]).then_inc(rden_done, 1)
                wait(dve, o_done, 2 * unit(b, off))
                wait(dve, rden_done, 2 * upto(b, off))
                dve.tensor_tensor(rscale[:, :], rden[:, :], cur_vs[:, :], ALU.mult).then_inc(rscale_done, 1)
                wait(dve, rscale_done, upto(b, off))
                wait(dve, o_turned, unit(b, off))
                for h in range(2):
                    hs = slice(HALF * h, HALF * (h + 1))
                    dve.tensor_tensor(o[:, hs, :], heads[:, h, :, 0:DH],
                                      rscale[:, hs].unsqueeze(2).to_broadcast([P, HALF, DH]), ALU.mult)\
                       .then_inc(o_done, 1)

            def result(b, off):
                if not exists(b, off):
                    return
                s = off % 4
                wait(dve, out_mm, upto(b, off))
                wait(dve, xr_ready, upto(b, off))
                dve.tensor_tensor(xr[:, s, :], ps_o[:, :], xr[:, s, :], ALU.add).then_inc(y_ready, 1)

            def softmax_shift(b, off):
                if not exists(b, off):
                    return
                for h in range(2):
                    wait(dve, s_mm, 2 * unit(b, off) + h + 1)
                    if h == 0:
                        wait(dve, sub_done, 2 * unit(b, off))
                    dve.tensor_reduce(mx[:, HALF * h:HALF * (h + 1)],
                                      ps_s[:, h, :].rearrange("p (h l) -> p h l", l=LKV), AX_X, ALU.max)\
                       .then_inc(mx_done, 1)
                wait(dve, p_turned, 2 * unit(b, off))
                for h in range(2):
                    hs = slice(HALF * h, HALF * (h + 1))
                    wait(dve, mx_done, 2 * unit(b, off) + h + 1)
                    dve.tensor_tensor(pr[:, hs, :], ps_s[:, h, :].rearrange("p (h l) -> p h l", l=LKV),
                                      mx[:, hs].unsqueeze(2).to_broadcast([P, HALF, LKV]), ALU.subtract)\
                       .then_inc(sub_done, 1)

            def turned_p(b, off, h):
                if not exists(b, off):
                    return
                wait(dve, pt_hi_done, 2 * unit(b, off) + h + 1)
                dve.tensor_tensor(pt_lo[:, 4 * h:4 * h + 4, :], ps_t[:, h, :].rearrange("p (g n) -> p g n", g=4),
                                  pt_hi[:, 4 * h:4 * h + 4, :], ALU.subtract).then_inc(pt_done, 1)

            def query(b, off):
                if not exists(b, off):
                    return
                s, m = (off // 4) % 2, off % 4
                wait(dve, q_hi_done, upto(b, off))
                dve.scalar_tensor_tensor(out=q_lo[:, s, m, :], in0=ps_q[:, :], scalar=cur_bq[:, m:m + 1],
                                         in1=q_hi[:, s, m, :].bitcast(F32), op0=ALU.add, op1=ALU.subtract)\
                   .then_inc(q_done, 1)

            def scaled_wq_lo(b, m):
                if not batch_exists(b):
                    return
                wait(dve, w_hi_done, KC * b + m + 1)
                cols = slice(P * m, P * (m + 1))
                dve.tensor_tensor(w_lo[:, :, cols], w_tmp[:, :, :], w_hi[:, :, cols].bitcast(F32), ALU.subtract)\
                   .then_inc(w_done, 1)

            def step(b, i):
                stats(b, i + 8)
                await_stats(b, i + 8)
                turned_x(b, i + 7)
                mean_var(b, i + 8)
                turned_o(b, i - 3)
                if i == 2 and batch_exists(b):
                    wait(dve, rscale_done, unit(b, 0))
                    dve.tensor_copy(cur_vs[:, :], v_scale_b[:, b, :]).then_inc(vs_staged, 1)
                    wait(dve, vs_staged, b + 1)
                normalise_o(b, i - 2)
                result(b, i - 4)
                softmax_shift(b, i)
                turned_p(b, i - 1, 0)
                turned_p(b, i - 1, 1)
                query(b, i + 4)
                if isinstance(b, int) and b == 0 and 1 <= i <= 2:
                    if i == 1:
                        output_bias()
                    wp_low(i - 1)
                if 1 <= i <= 4:
                    scaled_wq_lo(b + 1, i - 1)

            def wp_low(part):
                dve.wait_ge(wp_hi_done, part + 1)
                ks = slice(KC // 2 * part, KC // 2 * (part + 1))
                dve.tensor_tensor(wp_lo[:, ks, :], wp_raw[:, ks, :], wp_hi[:, ks, :].bitcast(F32), ALU.subtract)\
                   .then_inc(wp_ready, 1)

            def output_bias():
                dve.wait_ge(bv_mm, 1)
                dve.wait_ge(ld_bp, 16)
                dve.tensor_tensor(bp_row[:, :], ps_o[:, :], bp_row[:, :], ALU.add).then_inc(bias_ready, 1)

            def prime():
                def all_stats(f):
                    stats(0, f)
                    await_stats(0, f)
                    mean_var(0, f)

                for n in range(2 * KC):
                    half, k = n // KC, n % KC
                    seg = turned[n % TURNED].rearrange("p (b l) -> p b l", b=BH)
                    sc = sc_kv[:, k, BH * half:BH * (half + 1)].unsqueeze(2).to_broadcast([P, BH, LKV])
                    sh = sh_kv[:, k, BH * half:BH * (half + 1)].unsqueeze(2).to_broadcast([P, BH, LKV])
                    if n == 0:
                        dve.wait_ge(mod_ready, 2)
                    dve.wait_ge(cx_turned, n + 1)
                    wait(dve, cT_done, n - TURNED + 1)
                    dve.tensor_tensor(seg, ps_t[:, n % 2, :].rearrange("p (b l) -> p b l", b=BH), sc, ALU.mult)\
                       .then_inc(c_mul, 1)
                    dve.wait_ge(c_mul, n + 1)
                    dve.tensor_tensor(seg, seg, sh, ALU.add).then_inc(c_mod, 1)
                    if n == 0:
                        modulation(1)
                    if n in (5, 6):
                        all_stats(n - 5)
                    if n > KC:
                        scaled_wq_lo(0, n - KC - 1)
                    if n == KC:
                        dve.wait_ge(wk_hi_done, 1)
                        dve.tensor_tensor(wk_lo, wk_raw, wk_hi.bitcast(F32), ALU.subtract).then_inc(wk_done, 1)

                dve.wait_ge(bq_mm, KC)
                dve.tensor_tensor(bqT[:].rearrange("p b m -> p m b"),
                                  ps_q[:, 0:KC * B].rearrange("p (m b) -> p m b", b=B),
                                  bias_t[:, BQ:BQ + KC].unsqueeze(2).to_broadcast([P, KC, B]), ALU.add)\
                   .then_inc(bq_ready, 1)

                scaled_wq_lo(0, KC - 1)
                dve.tensor_copy(bv_cols, bias_t[:, BV:BV + KC].unsqueeze(2).to_broadcast([P, KC, P]))\
                   .then_inc(bv_spread, 1)
                for t in range(CT + 1):
                    if t < CT:
                        value_max(t)
                    if 1 <= t <= 6:
                        all_stats(t + 1)
                    if t > 0:
                        keys(t - 1)
                    if t < CT:
                        value_power(t)
                    if t == CT - 1:
                        turned_x(0, KC)
                    if t > 0:
                        value_place(t - 1)
                    if 1 <= t <= KC:
                        turned_x(0, t - 1)
                    if t == CT - 1:
                        turned_x(0, KC + 1)
                    if t == CT:
                        turned_x(0, KC + 2)
                    if t > KC:
                        query(0, t - KC - 1)
                dve.tensor_copy(v_scale_b[:].rearrange("p (t e) h -> p t e h", e=2),
                                v_scale[:].unsqueeze(2).to_broadcast([P, CT, 2, NH])).then_inc(vs_spread, 1)
                dve.wait_ge(vs_spread, 1)

            every_step(dve, step, prime)

        @block.tensor
        def _(pe):
            pe.wait_ge(id_ready, 1)
            pe.wait_ge(ld_small, 16 * 5)
            pe.transpose(ps_t[:, 0, 0:7 * KC], brow, ident[0:7 * KC, 0:7 * KC]).then_inc(small_turned, 1)
            for k in range(KC):
                last = pe.transpose(ps_t[:, 1, B * k:B * (k + 1)], c_row[:, P * k:P * (k + 1)], ident[0:B, 0:B])
            last.then_inc(small_turned, 1)

            pe.wait_ge(silu_step, 3)
            def modulate(side, landed):
                for k in range(KC):
                    pe.wait_ge(landed[k], 16)
                    for a in range(2):
                        last = pe.matmul((ps_s, ps_v)[side][0:B, a, :], silu_t[:, k, :],
                                         wss[side][:, k, H * a:H * (a + 1)], start=(k == 0), stop=(k == KC - 1))
                last.then_inc(mod_mm, 1)

            def turn_modulation(side):
                pe.wait_ge(mod_copied, side + 1)
                for m in range(2 * KC):
                    last = pe.transpose(ps_t[:, side, B * m:B * (m + 1)], mod_rows[side][:, P * m:P * (m + 1)],
                                        ident[0:B, 0:B])
                last.then_inc(mod_turned, 1)

            def turn_context(n):
                half, k = n // KC, n % KC
                wait(pe, c_mul, n - 1)
                for t in range(4):
                    pe.wait_ge(cx_ready, 4 * half + t + 1)
                    last = pe.transpose(ps_t[:, n % 2, P * t:P * (t + 1)], cx[:, 4 * half + t, P * k:P * (k + 1)],
                                        ident[:, :])
                last.then_inc(cx_turned, 1)

            def shift_product(m):
                for k in range(KC):
                    last = pe.matmul(ps_q[:, B * m:B * (m + 1)], wq[:, k, P * m:P * (m + 1)], sh_q[:, k, :],
                                     start=(k == 0), stop=(k == KC - 1))
                last.then_inc(bq_mm, 1)

            modulate(0, ld_ss)
            turn_modulation(0)
            modulate(1, ld_ssq)
            pe.wait_ge(mod_ready, 2)
            turn_context(0)
            turn_modulation(1)
            pe.wait_ge(mod_ready, 4)
            pe.wait_ge(ld_wq, 16)
            for m in range(KC):
                turn_context(m + 1)
                shift_product(m)
            turn_context(5)

            def split_product(dst, terms):
                last = None
                for n, (a, b) in enumerate((terms(p, k) for p in ((0, 0), (0, 1), (1, 0)) for k in range(KC))):
                    last = pe.matmul(dst, a, b, start=(n == 0), stop=(n == 3 * KC - 1))
                return last

            def value_rows(t):
                wait(pe, v_copied, t - 1)
                half, cols = t // 4, slice(P * (t % 4), P * (t % 4 + 1))
                split_product(ps_s[:, t % 2, :], lambda p, k: (
                    (cT_hi, cT_lo)[p[0]][half][:, k, cols], (wv_hi, wv_lo)[p[1]][:, k, :])).then_inc(v_mm, 1)

            def key_rows(n):
                half, m = n // KC, n % KC
                wait(pe, k_ready, n - 1)
                split_product(ps_v[:, n % 2, :], lambda p, k: (
                    (wk_hi, wk_lo)[p[0]][:, k, P * m:P * (m + 1)],
                    (cT_hi, cT_lo)[p[1]][half][:, k, :])).then_inc(k_mm, 1)

            def bias_product():
                pe.wait_ge(bv_spread, 1)
                pe.wait_ge(ld_wp, 16)
                for k in range(KC):
                    last = pe.matmul(ps_o[:, :], bv_cols[:, k, :], wp_raw[:, k, :], start=(k == 0), stop=(k == KC - 1))
                last.then_inc(bv_mm, 1)

            def turn_x(b, off):
                if not exists(b, off):
                    return
                wait(pe, xh_ready, upto(b, off))
                wait(pe, xT_done, unit(b, off))
                wait(pe, pt_done, 2 * unit(b, off - 9) + 1)
                for k in range(KC):
                    last = pe.transpose(ps_t[:, 0, P * k:P * (k + 1)], xh[:, off % 2, P * k:P * (k + 1)], ident[:, :])
                last.then_inc(xT_turned, 1)

            def project(b, off):
                if not exists(b, off):
                    return
                s, m = (off // 4) % 2, off % 4
                if m == 0:
                    wait(pe, xT_done, upto(b, off + 3))
                if off % PER < 4:
                    wait(pe, w_done, KC * (b + off // PER) + m + 1)
                wait(pe, q_done, unit(b, off))
                cols = slice(P * m, P * (m + 1))
                n = 0
                for w, xt in ((w_hi, xT_hi), (w_hi, xT_lo), (w_lo, xT_hi)):
                    for k in range(KC):
                        last = pe.matmul(ps_q[:, :], w[:, k, cols], xt[:, s, k, :], start=(n == 0),
                                         stop=(n == 3 * KC - 1))
                        n += 1
                last.then_inc(q_mm, 1)

            def score(b, off):
                if not exists(b, off):
                    return
                s = (off // 4) % 2
                cols = slice(P * (off % 4), P * (off % 4 + 1))
                if off % 4 == 0:
                    wait(pe, q_done, upto(b, off + 3))
                if off % PER == 0:
                    wait(pe, kb_done, HPG * (b + 1))
                for g in range(KC):
                    if g % 2 == 0:
                        wait(pe, sub_done, 2 * unit(b, off - 1) + g // 2 + 1)
                    dst = ps_s[:, g // 2, 256 * (g % 2):256 * (g % 2 + 1)]
                    for n, (qt, kt) in enumerate(((q_hi, kb_hi), (q_hi, kb_lo), (q_lo, kb_hi))):
                        last = pe.matmul(dst, qt[:, s, g, cols], kt[:, g, :, :].rearrange("p h l -> p (h l)"),
                                         start=(n == 0), stop=(n == 2))
                    if g % 2 == 1:
                        last.then_inc(s_mm, 1)

            def turn_p(b, off):
                if not exists(b, off):
                    return
                wait(pe, exp_done, upto(b, off))
                for h in range(2):
                    if h == 0:
                        wait(pe, xT_done, upto(b, off + 8))
                    else:
                        wait(pe, oT_done, unit(b, off - 1))
                    wait(pe, pt_done, 2 * unit(b, off - 1) + h + 1)
                    for g in range(4):
                        pair = 4 * h + g
                        last = pe.transpose(ps_t[:, h, P * g:P * (g + 1)],
                                            pr[:, 2 * pair:2 * pair + 2, :].rearrange("p h l -> p (h l)"),
                                            ident[:, :])
                    last.then_inc(p_turned, 1)

            def weigh(b, off):
                if not exists(b, off):
                    return
                if off % PER == 0:
                    wait(pe, vb_done, 4 * (b + off // PER + 1))
                wait(pe, o_done, 2 * unit(b, off))
                for h in range(2):
                    wait(pe, pt_done, 2 * unit(b, off) + h + 1)
                    for g in range(4):
                        pair = 4 * h + g
                        dst = ps_v[:, h, 2 * VC * g:2 * VC * (g + 1)]
                        for n, (pt, part) in enumerate(((pt_hi, 0), (pt_hi, 1), (pt_lo, 0))):
                            last = pe.matmul(dst, pt[:, pair, :],
                                             vb[:, part, pair, :, :].rearrange("p h c -> p (h c)"),
                                             start=(n == 0), stop=(n == 2))
                    last.then_inc(pv_mm, 1)

            def turn_o(b, off):
                if not exists(b, off):
                    return
                wait(pe, o_done, 2 * upto(b, off))
                wait(pe, oT_done, unit(b, off))
                wait(pe, pt_done, 2 * upto(b, off + 1))
                for k in range(KC):
                    last = pe.transpose(ps_t[:, 1, P * k:P * (k + 1)],
                                        o[:, HPG * k:HPG * (k + 1), :].rearrange("p h d -> p (h d)"), ident[:, :])
                last.then_inc(o_turned, 1)

            def project_out(b, off):
                if not exists(b, off):
                    return
                if isinstance(b, int) and b == 0:
                    wait(pe, wp_ready, 2)
                wait(pe, oT_done, upto(b, off))
                wait(pe, y_ready, unit(b, off))
                n = 0
                for ot, w in ((oT_hi, wp_hi), (oT_hi, wp_lo), (oT_lo, wp_hi)):
                    for k in range(KC):
                        last = pe.matmul(ps_o[:, :], ot[:, k, :], w[:, k, :], start=(n == 0), stop=(n == 3 * KC - 1))
                        n += 1
                last.then_inc(out_mm, 1)

            def step(b, i):
                score(b, i)
                turn_p(b, i - 1)
                project(b, i + 4)
                project_out(b, i - 3)
                turn_x(b, i + 8)
                turn_o(b, i - 2)
                weigh(b, i - 1)
                if isinstance(b, int) and b == 0 and i == 0:
                    bias_product()

            def prime():
                pe.wait_ge(cT_done, KC)
                pe.wait_ge(wv_done, 1)
                value_rows(0)
                turn_context(6)
                turn_context(7)
                pe.wait_ge(wk_done, 1)
                key_rows(0)
                for n in range(1, CT):
                    if n == KC:
                        pe.wait_ge(cT_done, 2 * KC)
                    value_rows(n)
                    if n == CT - 1:
                        turn_x(0, KC)
                    key_rows(n)
                    if n <= KC:
                        turn_x(0, n - 1)
                    if n == CT - 1:
                        turn_x(0, KC + 1)
                    if n == KC + 1:
                        pe.wait_ge(bq_ready, 1)
                    if n > KC:
                        project(0, n - KC - 1)
                turn_x(0, KC + 2)
                project(0, KC - 1)
                turn_x(0, KC + 3)

            every_step(pe, step, prime)


_INS = ["x", "ctx_1024", "cond_1024", "L0_xcond_Wq", "L0_xcond_bq", "L0_xcond_Wkv", "L0_xcond_bkv", "L0_xcond_Wp",
        "L0_xcond_bp", "L0_xcond_Wss_q", "L0_xcond_bss_q", "L0_xcond_Wss_kv", "L0_xcond_bss_kv"]
_OUTS = [((16, 1024, 512), "float32")]


def kernel(**inputs):
    import numpy as _np
    import concourse.bacc as _bacc
    from concourse import mybir as _mybir
    from concourse.bass_utils import run_bass_kernel_spmd as _run

    nc = _bacc.Bacc("TRN2", target_bir_lowering=False, num_devices=1)
    arrays, args = {}, []
    for name in _INS:
        a = _np.ascontiguousarray(inputs[name])
        arrays[f"in_{name}_dram"] = a
        args.append(nc.dram_tensor(f"in_{name}_dram", a.shape, _mybir.dt.from_np(a.dtype), kind="ExternalInput").ap())
    for i, (shape, dtype) in enumerate(_OUTS):
        dt = _mybir.dt.from_np(_np.dtype(dtype))
        args.append(nc.dram_tensor(f"out_{i}_dram", shape, dt, kind="ExternalOutput").ap())
    adaln_cross_attention(nc, *args)
    r = _run(nc, [arrays], core_ids=[0])
    return r.results[0]["out_0_dram"]
```

```python
from contextlib import ExitStack

import concourse.bass as bass
from concourse import mybir

ALU = mybir.AluOpType
ACT = mybir.ActivationFunctionType
F32 = mybir.dt.float32
F32R = mybir.dt.float32r
F16 = mybir.dt.float16
U32 = mybir.dt.uint32
AX_X = mybir.AxisListType.X

P = 128
EPS = 1e-5
EXPONENT_BITS = 0x7F800000
TOP = 2.0 ** 14


def adaln_cross_attention(nc, x, ctx_in, cond, Wq, bq, Wkv, bkv, Wp, bp, Wss_q, bss_q, Wss_kv, bss_kv, out):
    B, LQ, H = x.shape
    LKV = ctx_in.shape[1]
    DH = 32
    NH = H // DH
    KC = H // P
    PER = LQ // P
    TILE = 4
    UNITS = B * PER
    PAIRS = NH // 2
    HPG = P // DH
    VC = DH + 1
    CT = B * LKV // P
    HALF = NH // 2
    BH = 8
    assert P == 2 * LKV and H == 512 and PER == 2 * TILE and NH == KC * HPG

    with ExitStack() as ctx:
        def sb(name, shape, dt, stack=ctx):
            return stack.enter_context(nc.sbuf_tensor(name, shape, dt))

        def psum(name, shape):
            return ctx.enter_context(nc.psum_tensor(name, shape, F32))

        def sem(name):
            return ctx.enter_context(nc.semaphore(name))

        ps_s = psum("ps_s", [P, 2, 512])
        ps_t = psum("ps_t", [P, 2, 512])
        ps_q = psum("ps_q", [P, 512])
        ps_o = psum("ps_o", [P, 512])
        ps_v = psum("ps_v", [P, 2, 512])

        first_banks = (ps_q, ps_o)

        ident = sb("ident", [P, P], F32)
        wq = sb("wq", [P, KC, H], F32)
        wp_hi = sb("wp_hi", [P, KC, H], F32R)
        wp_lo = sb("wp_lo", [P, KC, H], F32R)
        w_tmp = sb("w_tmp", [P, KC, P], F32)
        w_hi = sb("w_hi", [P, KC, H], F32R)
        w_lo = sb("w_lo", [P, KC, H], F32R)
        with ExitStack() as scratch:
            cx = sb("cx", [P, CT, H], F32, scratch)[:, :, :]
        k16 = sb("k16", [P, B, 2, KC, LKV], F16)
        kb = sb("kb", [P, 2, PAIRS, 2, LKV], F16)
        v_all = sb("v_all", [P, 2, B, PAIRS, DH], F16)
        vb = sb("vb", [P, 2, PAIRS, 2, VC], F16)
        v_scale = sb("v_scale", [P, CT, NH], F32)
        v_inv = sb("v_inv", [P, CT, NH], F32)
        bp_row = sb("bp_row", [P, H], F32)
        bqT = sb("bqT", [P, B, KC], F32)
        one_sc = sb("one_sc", [P, B, KC], F32)
        lim = sb("lim", [P, 8], F32)
        lim_all = sb("lim_all", [P, 8], F32)
        lim_f = sb("lim_f", [P, 2], F32)
        lim_sum = sb("lim_sum", [P, 2], F32)
        qk_scale = sb("qk_scale", [P, 2], F32)
        exp_scale = sb("exp_scale", [P, 1], F32)
        one_half = sb("one_half", [P, 2], F32)
        y = sb("y", [P, 2, H], F32)
        cur_bq = sb("cur_bq", [P, KC], F32)
        cur_sc = sb("cur_sc", [P, KC], F32)
        cur_vs = sb("cur_vs", [P, NH], F32)
        v_scale_b = sb("v_scale_b", [P, B, NH], F32)
        half_neg = sb("half_neg", [P, CT], F32)
        x_in = sb("x_in", [P, 4, H], F32)
        xr = sb("xr", [P, 4, H], F32)
        st = sb("st", [P, 6], F32)
        mv = sb("mv", [P, 2, 2], F32)
        nmv = sb("nmv", [P, 2, 2], F32)
        sign = sb("sign", [P, 2], F32)
        eps = sb("eps", [P, 1], F32)
        veps = sb("veps", [P, 2], F32)
        rstd = sb("rstd", [P, 2], F32)
        xh = sb("xh", [P, 2, H], F32)
        first_rows = sb("first_rows", [P, 2, H], F32)
        pt_hi = sb("pt_hi", [P, PAIRS, P], F16)
        pt_lo = sb("pt_lo", [P, PAIRS, P], F16)
        mx = sb("mx", [P, NH], F32)
        rden = sb("rden", [P, NH], F32)
        rscale = sb("rscale", [P, NH], F32)
        o = sb("o", [P, NH, DH], F32)
        oT_hi = sb("oT_hi", [P, KC, P], F32R)
        oT_lo = sb("oT_lo", [P, KC, P], F32R)

        BSSQ, BSSKV, BQ, BK, BV = 0, 2 * KC, 4 * KC, 5 * KC, 6 * KC
        row_slots = first_rows[:, :, :]
        o_slot = o[:].rearrange("p h d -> p (h d)")
        brow = o_slot[0:7 * KC, 0:P]
        c_row = row_slots[0:B, 0, :]
        v16 = [t[:].rearrange("p g n -> p (g n)").rearrange("p (s n) -> p s n", s=2) for t in (pt_hi, pt_lo)]
        bv_cols = o_slot.rearrange("p (k n) -> p k n", k=KC)
        bias_t = sb("bias_t", [P, 7 * KC], F32)
        c_t = sb("c_t", [P, KC, B], F32)
        silu_t = sb("silu_t", [P, KC, B], F32)
        sig_t = sb("sig_t", [P, KC, B], F32)
        sh_q = sb("sh_q", [P, KC, B], F32)
        sc_kv = sb("sc_kv", [P, KC, B], F32)
        sh_kv = sb("sh_kv", [P, KC, B], F32)
        cst = sb("cst", [P, CT, 6], F32)
        cmv = sb("cmv", [P, CT, 2], F32)
        cveps = sb("cveps", [P, CT], F32)
        crstd = sb("crstd", [P, CT], F32)

        with ExitStack() as scratch:
            raw = sb("raw", [P, 8, KC * H], F32, scratch)
        xT_hi = sb("xT_hi", [P, 2, KC, 512], F32R)
        xT_lo = sb("xT_lo", [P, 2, KC, 512], F32R)
        qs = sb("qs", [P, 2, PAIRS, 512], F16)
        ctx_hi = sb("ctx_hi", [P, 2, KC, 512], F32R)
        with ExitStack() as scratch:
            ctx_lo = sb("ctx_lo", [P, 2, KC, 512], F32R, scratch)
        pr = sb("pr", [P, 2, NH, LKV], F32)
        wk_raw = raw[:, 0, :].rearrange("p (k n) -> p k n", k=KC)
        wv_raw = raw[:, 2, :].rearrange("p (k n) -> p k n", k=KC)
        wss = [raw[:, 4 + 2 * a:6 + 2 * a, :].rearrange("p a n -> p (a n)").rearrange("p (k n) -> p k n", k=KC)
               for a in range(2)]
        mod_rows = [raw[0:B, at, 0:2 * H] for at in (1, 5)]
        TURNED = 3
        turned = [raw[:, 4, H * a:H * (a + 1)] for a in range(TURNED)]
        k32 = [raw[:, 5, 2 * H + H * a:3 * H + H * a] for a in range(2)]
        wv_hi, wv_lo = xT_hi[:, 1], xT_lo[:, 1]
        wk_hi, wk_lo = wp_hi[:, :, :], wp_lo[:, :, :]
        cT_hi = [ctx_hi[:, 0], ctx_hi[:, 1]]
        cT_lo = [ctx_lo[:, 0], ctx_lo[:, 1]]
        squares = wp_lo[:, :, :]
        wp_raw = xr[:, :, :]

        ld_small, ld_ctx, ld_wv, ld_wk, ld_wq, ld_wp, ld_bp = (
            sem(n) for n in ("ld_small", "ld_ctx", "ld_wv", "ld_wk", "ld_wq", "ld_wp", "ld_bp"))
        ld_ss = [sem(f"ld_ss{k}") for k in range(KC)]
        ld_ssq = [sem(f"ld_ssq{k}") for k in range(KC)]
        id_zero, id_ready, zeros_ready, consts_ready, bd_ready = (
            sem(n) for n in ("id_zero", "id_ready", "zeros_ready", "consts_ready", "bd_ready"))
        small_turned, c_copied, c_exp, silu_step, mod_mm, mod_copied, mod_turned, mod_ready = (
            sem(n) for n in ("small_turned", "c_copied", "c_exp", "silu_step", "mod_mm", "mod_copied", "mod_turned",
                             "mod_ready"))
        bq_mm, bq_ready = sem("bq_mm"), sem("bq_ready")
        c_stats, c_mv, c_pool, cx_ready, cx_turned, c_mul, c_mod, cT_hi_done, cT_done = (
            sem(n) for n in ("c_stats", "c_mv", "c_pool", "cx_ready", "cx_turned", "c_mul", "c_mod", "cT_hi_done",
                             "cT_done"))
        wv_hi_done, wv_done, wk_hi_done, wk_done = (
            sem(n) for n in ("wv_hi_done", "wv_done", "wk_hi_done", "wk_done"))
        k_mm, k_ready, v_mm, v_copied, v_max, v_red, v_step, v_scaled, v_hi_done, v_lo_done, v_hi_placed, v_placed = (
            sem(n) for n in ("k_mm", "k_ready", "v_mm", "v_copied", "v_max", "v_red", "v_step", "v_scaled",
                             "v_hi_done", "v_lo_done", "v_hi_placed", "v_placed"))
        squared, lim_done, lim_red, lim_step, k32_done, k_hi_done = (
            sem(n) for n in ("squared", "lim_done", "lim_red", "lim_step", "k32_done", "k_hi_done"))
        wp_hi_done, wp_ready, bv_spread, bv_mm, bias_ready = (
            sem(n) for n in ("wp_hi_done", "wp_ready", "bv_spread", "bv_mm", "bias_ready"))

        x_loaded = [sem(f"x_loaded{i}") for i in range(4)]
        xr_loaded = [sem(f"xr_loaded{i}") for i in range(4)]
        stored = [sem(f"stored{i}") for i in range(4)]
        ln_bn, ln_mv, ln_step, xh_ready, xT_turned, xT_hi_done, xT_done = (
            sem(n) for n in ("ln_bn", "ln_mv", "ln_step", "xh_ready", "xT_turned", "xT_hi_done", "xT_done"))
        sc_staged, w_tmp_done, w_hi_done, w_done = (
            sem(n) for n in ("sc_staged", "w_tmp_done", "w_hi_done", "w_done"))
        bq_staged, q_mm, q_hi_done, q_done = (
            sem(n) for n in ("bq_staged", "q_mm", "q_hi_done", "q_done"))
        kb_dve_done, kb_act_done, vb_done, vs_staged = (
            sem(n) for n in ("kb_dve_done", "kb_act_done", "vb_done", "vs_staged"))
        s_mm, mx_done, sub_done, exp_done, p_turned, pt_hi_done, pt_done = (
            sem(n) for n in ("s_mm", "mx_done", "sub_done", "exp_done", "p_turned", "pt_hi_done", "pt_done"))
        pv_mm, rden_done, rscale_done, o_done, o_turned, oT_hi_done, oT_done = (
            sem(n) for n in ("pv_mm", "rden_done", "rscale_done", "o_done", "o_turned", "oT_hi_done", "oT_done"))
        vs_spread = sem("vs_spread")
        out_mm, xr_ready, y_copied, y_ready = sem("out_mm"), sem("xr_ready"), sem("y_copied"), sem("y_ready")

        SCALED_SC, EXP_SCALED = 7, 10

        x_units = x.rearrange("b (i p) d -> (b i) p d", p=P)
        out_units = out.rearrange("b (i p) d -> (b i) p d", p=P)

        def wait(eng, s, n):
            if not isinstance(n, int) or n > 0:
                eng.wait_ge(s, n)

        def unit(b, off):
            return PER * b + off

        def exists(b, off):
            return not isinstance(b, int) or 0 <= PER * b + off < UNITS

        def upto(b, off):
            n = PER * b + off + 1
            return min(max(n, 0), UNITS) if isinstance(b, int) else n

        def batch_exists(b):
            return not isinstance(b, int) or b < B

        def every_step(eng, step, prime=None):
            if prime:
                prime()
            for i in range(PER):
                step(0, i)
            with eng.Fori(1, B - 1) as b:
                for i in range(PER):
                    step(b, i)
            for i in range(PER):
                step(B - 1, i)
            for i in range(4):
                step(B, i)

        def bank_o(b, off):
            return 0 if isinstance(b, int) and PER * b + off >= PER * (B - 1) else 1

        def place(copy, part, t):
            for hb in range(2):
                for par in range(2):
                    src = v16[part][LKV * hb:LKV * (hb + 1), t % 2, :]\
                        .rearrange("p (g e d) -> p g e d", e=2, d=DH)[:, :, par, :]
                    last = copy(v_all[LKV * par:LKV * (par + 1), part, 2 * t + hb, :, :], src)
            return last

        block = ctx.enter_context(nc.Block())

        @block.sync
        def _(sp):
            sp.dma_start(c_row, cond).then_inc(ld_small, 16)
            for at, v, n in ((BSSQ, bss_q, 2 * KC), (BSSKV, bss_kv, 2 * KC), (BQ, bq, KC), (BK, bkv, 2 * KC)):
                sp.dma_start(brow[at:at + n, :], v.rearrange("(r c) -> r c", c=P)).then_inc(ld_small, 16)
            for k in range(KC):
                sp.dma_start(wss[0][:, k, :], Wss_kv[P * k:P * (k + 1), :]).then_inc(ld_ss[k], 16)
            sp.dma_start(cx, ctx_in.rearrange("b l d -> (b l) d").rearrange("(t p) d -> p t d", p=P)).then_inc(ld_ctx, 16)
            for k in range(KC):
                sp.dma_start(wss[1][:, k, :], Wss_q[P * k:P * (k + 1), :]).then_inc(ld_ssq[k], 16)
            sp.dma_start(wv_raw, Wkv[:, H:2 * H].rearrange("(k p) n -> p k n", p=P)).then_inc(ld_wv, 16)
            sp.dma_start(wq[:, :, :], Wq.rearrange("(k p) n -> p k n", p=P)).then_inc(ld_wq, 16)
            sp.dma_start(wk_raw, Wkv[:, 0:H].rearrange("(k p) n -> p k n", p=P)).then_inc(ld_wk, 16)
            sp.dma_start(bp_row[:, :], bp.rearrange("(a n) -> a n", a=1).partition_broadcast(P)).then_inc(ld_bp, 16)

            def load_x(b, off):
                if not exists(b, off):
                    return
                wait(sp, xh_ready, unit(b, off - 3))
                sp.dma_start(x_in[:, off % 4, :], x_units[unit(b, off)]).then_inc(x_loaded[off % 4], 16)

            def load_xr(b, off):
                if not exists(b, off):
                    return
                wait(sp, stored[off % 4], 16 * (2 * b + off // 4))
                sp.dma_start(xr[:, off % 4, :], x_units[unit(b, off)]).then_inc(xr_loaded[off % 4], 16)

            def step(b, i):
                load_x(b, i + 12)
                load_xr(b, i)

            for f in range(4):
                load_x(0, f)
            sp.dma_start(wp_raw, Wp.rearrange("(k p) n -> p k n", p=P)).then_inc(ld_wp, 16)
            for f in range(4, 12):
                load_x(0, f)
            sp.wait_ge(wp_ready, 2)
            sp.wait_ge(bv_mm, 1)
            for i in range(PER):
                step(0, i)
            with sp.Fori(1, B - 2) as b:
                for i in range(PER):
                    step(b, i)
            for b in (B - 2, B - 1):
                for i in range(PER):
                    step(b, i)

        @block.gpsimd
        def _(pool):
            pool.memset(ident[:, :], 0.0).then_inc(id_zero, 1)
            pool.wait_ge(id_zero, 1)
            pool.affine_select(out=ident[:, :], in_=ident[:, :], compare_op=ALU.not_equal, fill=1.0,
                               base=0, pattern=[[-1, P]], channel_multiplier=1).then_inc(id_ready, 1)
            pool.memset(half_neg[:, :], -0.5).then_inc(consts_ready, 1)
            pool.memset(eps[:, :], EPS).then_inc(consts_ready, 1)
            pool.memset(sign[:, 0:1], -1.0).then_inc(consts_ready, 1)
            pool.memset(sign[:, 1:2], 1.0).then_inc(consts_ready, 1)
            pool.memset(one_half[:, :], 0.5).then_inc(consts_ready, 1)
            pool.memset(kb[:, :, :, :, :], 0.0).then_inc(bd_ready, 1)
            pool.memset(vb[:, :, :, :, :], 0.0).then_inc(zeros_ready, 1)
            pool.wait_ge(zeros_ready, 1)
            for par in range(2):
                rows = slice(LKV * par, LKV * (par + 1))
                pool.memset(vb[rows, 0, :, par, DH:VC], 1.0).then_inc(bd_ready, 1)
                pool.wait_ge(bd_ready, 2 + par)

            pool.wait_ge(consts_ready, 5)
            for half in range(2):
                ts = slice(CT // 2 * half, CT // 2 * (half + 1))
                pool.wait_ge(c_mv, CT // 2 * (half + 1))
                pool.tensor_scalar(cveps[:, ts], cmv[:, ts, 1], EPS, 1.0, ALU.add, ALU.mult).then_inc(c_pool, 1)
                pool.wait_ge(c_pool, 2 * half + 1)
                pool.tensor_tensor(crstd[:, ts], cveps[:, ts], half_neg[:, ts], ALU.pow).then_inc(c_pool, 1)

            def context_lo(n):
                half, m = n // KC, n % KC
                pool.wait_ge(cT_hi_done, n + 1)
                pool.tensor_tensor(cT_lo[half][:, m, :], turned[n % TURNED], cT_hi[half][:, m, :].bitcast(F32),
                                   ALU.subtract).then_inc(cT_done, 1)

            def value_scale(t):
                pool.wait_ge(v_max, t + 1)
                pool.partition_all_reduce(v_scale[:, t, :], v_inv[:, t, :], P,
                                          bass.bass_isa.ReduceOp.max).then_inc(v_red, 1)
                pool.wait_ge(v_step, 3 * (t + 1))
                rows = row_slots[:, t % 2, :].rearrange("p (h d) -> p h d", d=DH)
                pool.tensor_tensor(rows, rows, v_inv[:, t, :].unsqueeze(2).to_broadcast([P, NH, DH]), ALU.mult)\
                    .then_inc(v_scaled, 1)

            def moments(b, off):
                if not exists(b, off):
                    return
                s = off % 2
                wait(pool, xh_ready, unit(b, off - 1))
                wait(pool, ln_mv, upto(b, off))
                pool.tensor_tensor(nmv[:, s, :], mv[:, s, :], sign[:, :], ALU.mult).then_inc(ln_step, 1)
                wait(pool, ln_step, 3 * unit(b, off) + 1)
                pool.tensor_tensor(veps[:, s:s + 1], nmv[:, s, 1:2], eps[:, :], ALU.add).then_inc(ln_step, 1)
                wait(pool, ln_step, 3 * unit(b, off) + 2)
                pool.tensor_tensor(rstd[:, s:s + 1], veps[:, s:s + 1], half_neg[:, 0:1], ALU.pow)\
                    .then_inc(ln_step, 1)

            def await_moments(b, off):
                if exists(b, off):
                    wait(pool, xT_turned, unit(b, off - 1))
                    wait(pool, ln_step, 3 * upto(b, off))

            def normalise(b, off):
                if exists(b, off):
                    s = off % 2
                    pool.tensor_scalar(xh[:, s, :], x_in[:, off % 4, :], nmv[:, s, 0:1], rstd[:, s:s + 1],
                                       ALU.add, ALU.mult).then_inc(xh_ready, 1)

            def residual(b, off):
                if exists(b, off):
                    s = off % 4
                    wait(pool, bias_ready, 1)
                    wait(pool, xr_loaded[s], 16 * (2 * b + off // 4 + 1))
                    pool.tensor_tensor(xr[:, s, :], xr[:, s, :], bp_row[:, :], ALU.add).then_inc(xr_ready, 1)

            def scaled_wq(b, m):
                if not batch_exists(b):
                    return
                if m == 0:
                    wait(pool, lim_step, SCALED_SC)
                    wait(pool, w_tmp_done, KC * b)
                    pool.tensor_copy(cur_sc[:, :], one_sc[:, b, :]).then_inc(sc_staged, 1)
                    wait(pool, sc_staged, b + 1)
                wait(pool, w_done, KC * b + m)
                if m == 0 and isinstance(b, int) and b == 0:
                    pool.wait_ge(ld_wq, 16)
                pool.tensor_tensor(w_tmp[:, :, :], wq[:, :, m * P:(m + 1) * P],
                                   cur_sc[:, :].unsqueeze(2).to_broadcast([P, KC, P]), ALU.mult)\
                    .then_inc(w_tmp_done, 1)

            def add_rows(b, off):
                if exists(b, off):
                    s = off % 4
                    wait(pool, y_copied, upto(b, off))
                    wait(pool, xr_ready, upto(b, off))
                    pool.tensor_tensor(xr[:, s, :], y[:, off % 2, :], xr[:, s, :], ALU.add).then_inc(y_ready, 1)

            def scaled_wq_lo(b, m):
                if batch_exists(b):
                    wait(pool, w_hi_done, KC * b + m + 1)
                    cols = slice(P * m, P * (m + 1))
                    pool.tensor_tensor(w_lo[:, :, cols], w_tmp[:, :, :], w_hi[:, :, cols].bitcast(F32), ALU.subtract)\
                        .then_inc(w_done, 1)

            def key_lo(n):
                h, m = n // KC, n % KC
                pool.wait_ge(k_hi_done, n + 1)
                pool.tensor_tensor(k16[:, BH * h:BH * (h + 1), 1, m, :], k32[n % 2].rearrange("p (b l) -> p b l", b=BH),
                                   k16[:, BH * h:BH * (h + 1), 0, m, :], ALU.subtract).then_inc(k_ready, 1)

            def limits():
                pool.wait_ge(squared, 2)
                pool.wait_ge(lim_done, 6)
                pool.partition_all_reduce(lim_all[:, :], lim[:, :], P, bass.bass_isa.ReduceOp.max).then_inc(lim_red, 1)
                pool.wait_ge(lim_red, 1)
                pool.tensor_tensor(lim_f[:, :], lim_all[:, 0:2], one_half[:, :], ALU.pow).then_inc(lim_red, 1)

            def step(b, i):
                moments(b, i + 8)
                await_moments(b, i + 8)
                residual(b, i - 3)
                normalise(b, i + 8)
                add_rows(b, i - 4)
                if 2 <= i <= 5:
                    scaled_wq_lo(b + 1, i - 2)
                if 1 <= i <= 4:
                    scaled_wq(b + 1, i - 1)
                if isinstance(b, int) and b == 0 and i in (1, 2):
                    wp_low(i - 1)

            def wp_low(part):
                pool.wait_ge(wp_hi_done, part + 1)
                ks = slice(KC // 2 * part, KC // 2 * (part + 1))
                pool.tensor_tensor(wp_lo[:, ks, :], wp_raw[:, ks, :], wp_hi[:, ks, :].bitcast(F32), ALU.subtract)\
                    .then_inc(wp_ready, 1)

            def prime():
                def layernorm(f):
                    moments(0, f)
                    await_moments(0, f)
                    normalise(0, f)

                for n in range(2 * KC):
                    context_lo(n)
                    if n == KC:
                        limits()
                    if KC < n < KC + 3:
                        scaled_wq(0, n - KC - 1)
                for t in range(CT):
                    value_scale(t)
                    if t > 0:
                        key_lo(t - 1)
                    if t < 6:
                        layernorm(t)
                    if 5 <= t < 7:
                        scaled_wq(0, t - 3)
                layernorm(6)
                layernorm(7)
                key_lo(CT - 1)

            every_step(pool, step, prime)

        @block.scalar
        def _(act):
            act.wait_ge(c_copied, 1)
            act.activation(sig_t[:, :, :], c_t[:, :, :], ACT.Exp, scale=-1.0).then_inc(c_exp, 1)
            for side in range(2):
                act.wait_ge(mod_mm, side + 1)
                banks = (ps_s, ps_v)[side]
                act.copy(mod_rows[side].rearrange("b (a n) -> b a n", a=2), banks[0:B, :, :]).then_inc(mod_copied, 1)
            act.wait_ge(ld_wv, 16)
            act.wait_ge(mod_turned, 1)
            act.copy(wv_hi, wv_raw).then_inc(wv_hi_done, 1)

            def turned_x(b, off):
                if not exists(b, off):
                    return
                s = (off // 4) % 2
                cols = slice(P * (off % 4), P * (off % 4 + 1))
                wait(act, xT_turned, upto(b, off))
                if off % 4 == 0:
                    wait(act, q_mm, unit(b, off - 4))
                act.copy(xT_hi[:, s, :, cols], ps_t[:, 0, :].rearrange("p (k n) -> p k n", k=KC))\
                   .then_inc(xT_hi_done, 1)

            def turned_o(b, off):
                if not exists(b, off):
                    return
                wait(act, o_turned, upto(b, off))
                wait(act, out_mm, unit(b, off))
                act.copy(oT_hi[:, :, :], ps_t[:, bank_o(b, off), :].rearrange("p (k n) -> p k n", k=KC)).then_inc(oT_hi_done, 1)

            def key_twins(b):
                if not batch_exists(b):
                    return
                wait(act, s_mm, 2 * PER * b)
                for r in range(HPG):
                    to = slice(DH * ((r + 2) % HPG), DH * ((r + 2) % HPG + 1))
                    act.copy(kb[to, :, r // 2::2, r % 2, :], k16[DH * r:DH * (r + 1), b, :, :, :])\
                       .then_inc(kb_act_done, 1)
                act.copy(kb[0:DH, :, 0::2, 0, :], k16[0:DH, b, :, :, :]).then_inc(kb_act_done, 1)

            def output(b, off):
                if exists(b, off):
                    wait(act, out_mm, upto(b, off))
                    wait(act, y_ready, unit(b, off - 1))
                    act.copy(y[:, off % 2, :], ps_o[:, :]).then_inc(y_copied, 1)

            def values(b):
                if not batch_exists(b):
                    return
                wait(act, pv_mm, 2 * PER * b)
                for part in range(2):
                    for par in range(2):
                        rows = slice(LKV * par, LKV * (par + 1))
                        act.copy(vb[rows, part, :, par, 0:DH], v_all[rows, part, b, :, :]).then_inc(vb_done, 1)

            def query_bias(b):
                if not batch_exists(b):
                    return
                wait(act, q_done, 2 * PER * b)
                act.copy(cur_bq[:, :], bqT[:, b, :]).then_inc(bq_staged, 1)
                wait(act, bq_staged, b + 1)

            def turned_p(b, off, h):
                if not exists(b, off):
                    return
                wait(act, p_turned, 2 * unit(b, off) + h + 1)
                if h == 0:
                    wait(act, pv_mm, 2 * unit(b, off))
                act.copy(pt_hi[:, 4 * h:4 * h + 4, :], ps_t[:, h, :].rearrange("p (g n) -> p g n", g=4))\
                   .then_inc(pt_hi_done, 1)

            def query(b, off, bank=ps_q):
                if not exists(b, off):
                    return
                s, m = (off // 4) % 2, off % 4
                wait(act, q_mm, upto(b, off))
                if m == 0:
                    wait(act, s_mm, 2 * unit(b, off - 4))
                for pair in range(2):
                    rows = slice(64 * pair, 64 * (pair + 1))
                    act.activation(qs[rows, s, 2 * m + pair, :], bank[rows, :], ACT.Identity,
                                   bias=cur_bq[rows, m:m + 1]).then_inc(q_hi_done, 1)

            def scaled_wq_hi(b, m):
                if not batch_exists(b):
                    return
                wait(act, w_tmp_done, KC * b + m + 1)
                wait(act, q_mm, PER * (b - 1) + 4 + m + 1)
                act.copy(w_hi[:, :, m * P:(m + 1) * P], w_tmp[:, :, :]).then_inc(w_hi_done, 1)

            def step(b, i):
                if not (isinstance(b, int) and b == 0 and i == 0):
                    turned_x(b, i + 7)
                turned_o(b, i - 3)
                output(b, i - 4)
                if isinstance(b, int) and b == 0 and i in (1, 2):
                    wp_high(i - 1)
                if 2 <= i <= 5:
                    scaled_wq_hi(b + 1, i - 2)
                if i == 1:
                    values(b)
                if i == 4:
                    query_bias(b + 1)
                if i == 7:
                    key_twins(b + 1)
                query(b, i + 4)
                turned_p(b, i - 1, 0)
                turned_p(b, i - 1, 1)
                if exists(b, i):
                    if isinstance(b, int) and b == 0 and i == 0:
                        act.wait_ge(lim_step, EXP_SCALED)
                    wait(act, sub_done, 2 * upto(b, i))
                    act.activation(pr[:, i % 2], pr[:, i % 2], ACT.Exp, scale=exp_scale[:, 0:1]).then_inc(exp_done, 1)
                if exists(b, i - 4):
                    s = (i - 4) % 4
                    wait(act, y_ready, upto(b, i - 4))
                    act.dma_start(out_units[unit(b, i - 4)], xr[:, s, :]).then_inc(stored[s], 16)

            def wp_high(part):
                act.wait_ge(k_mm, 2 * KC)
                act.wait_ge(ld_wp, 16)
                ks = slice(KC // 2 * part, KC // 2 * (part + 1))
                act.copy(wp_hi[:, ks, :], wp_raw[:, ks, :]).then_inc(wp_hi_done, 1)

            def prime():
                for n in range(2 * KC):
                    act.wait_ge(c_mod, n + 1)
                    act.copy(cT_hi[n // KC][:, n % KC, :], turned[n % TURNED]).then_inc(cT_hi_done, 1)
                    if KC < n < KC + 3:
                        scaled_wq_hi(0, n - KC - 1)
                    if n == 0:
                        act.wait_ge(ld_wq, 16)
                        act.activation(squares, wq[:, :, :], ACT.Square, accum_out=lim[:, 0:1]).then_inc(squared, 1)
                    if n == KC - 1:
                        act.wait_ge(ld_wk, 16)
                        act.wait_ge(squared, 1)
                        act.activation(squares, wk_raw, ACT.Square, accum_out=lim[:, 1:2]).then_inc(squared, 1)
                        act.copy(wk_hi, wk_raw).then_inc(wk_hi_done, 1)
                act.wait_ge(wk_done, 1)
                for t in range(CT + 1):
                    if t < CT:
                        act.wait_ge(v_mm, t + 1)
                        wait(act, v_lo_done, t - 1)
                        act.copy(row_slots[:, t % 2, :], ps_s[:, t % 2, :]).then_inc(v_copied, 1)
                    if t == 6:
                        scaled_wq_hi(0, KC - 2)
                    if t == CT - 1:
                        turned_x(0, KC)
                    if t == CT:
                        query(0, 2, first_banks[0])
                        turned_x(0, KC + 2)
                        query(0, 3, first_banks[1])
                        turned_x(0, KC + 3)
                    if t > 0:
                        value_hi(t - 1)
                    if t > 0:
                        key_hi(t - 1)
                    if t == 7:
                        scaled_wq_hi(0, KC - 1)
                    if 2 <= t <= KC + 1:
                        turned_x(0, t - 2)
                    if t == KC + 1:
                        act.wait_ge(bq_ready, 2)
                        query_bias(0)
                        act.wait_ge(k_ready, KC)
                        act.wait_ge(bd_ready, 3)
                        key_twins(0)
                    if CT - 2 <= t < CT:
                        query(0, t - CT + 2, first_banks[t % 2])
                    if t == CT - 1:
                        turned_x(0, KC + 1)

            def key_hi(n):
                h, m = n // KC, n % KC
                act.wait_ge(k32_done, n + 1)
                act.copy(k16[:, BH * h:BH * (h + 1), 0, m, :], k32[n % 2].rearrange("p (b l) -> p b l", b=BH))\
                   .then_inc(k_hi_done, 1)

            def value_hi(t):
                act.wait_ge(v_scaled, t + 1)
                wait(act, v_placed, t - 1)
                wait(act, v_hi_placed, t - 1)
                act.copy(v16[0][:, t % 2, :], row_slots[:, t % 2, :]).then_inc(v_hi_done, 1)
                act.wait_ge(v_hi_done, t + 1)
                place(act.copy, 0, t).then_inc(v_hi_placed, 1)

            every_step(act, step, prime)
            for s in stored:
                act.wait_ge(s, 16 * (UNITS // 4))

        @block.vector
        def _(dve):
            dve.wait_ge(small_turned, 2)
            dve.tensor_copy(c_t[:, :, :], ps_t[:, 1, 0:KC * B].rearrange("p (k b) -> p k b", k=KC)).then_inc(c_copied, 1)
            dve.tensor_copy(bias_t[:, :], ps_t[:, 0, 0:7 * KC]).then_inc(c_copied, 1)
            dve.wait_ge(c_exp, 1)
            dve.tensor_scalar(sig_t[:, :, :], sig_t[:, :, :], 1.0, None, ALU.add).then_inc(silu_step, 1)
            dve.wait_ge(silu_step, 1)
            dve.reciprocal(sig_t[:, :, :], sig_t[:, :, :]).then_inc(silu_step, 1)
            dve.wait_ge(silu_step, 2)
            dve.wait_ge(c_copied, 2)
            dve.tensor_tensor(silu_t[:, :, :], sig_t[:, :, :], c_t[:, :, :], ALU.mult).then_inc(silu_step, 1)

            dve.wait_ge(ld_ctx, 16)
            for half in range(2):
                ts = range(CT // 2 * half, CT // 2 * (half + 1))
                for t in ts:
                    dve.bn_stats(cst[:, t, :], cx[:, t, :]).then_inc(c_stats, 1)
                for t in ts:
                    dve.wait_ge(c_stats, t + 1)
                    dve.bn_aggr(cmv[:, t, :], cst[:, t, :]).then_inc(c_mv, 1)
            def modulation(side):
                at, outs = ((BSSKV, (sc_kv[:, :, :], sh_kv[:, :, :])),
                            (BSSQ, (one_sc[:].rearrange("p b k -> p k b"), sh_q[:, :, :])))[side]
                dve.wait_ge(mod_turned, side + 1)
                ps = ps_t[:, side, 0:2 * KC * B].rearrange("p (m b) -> p m b", b=B)
                for part, (o_ap, plus) in enumerate(zip(outs, (1.0, 0.0))):
                    bias = bias_t[:, at + KC * part:at + KC * (part + 1)].unsqueeze(2).to_broadcast([P, KC, B])
                    dve.scalar_tensor_tensor(out=o_ap, in0=ps[:, KC * part:KC * (part + 1), :], scalar=plus,
                                             in1=bias, op0=ALU.add, op1=ALU.add).then_inc(mod_ready, 1)

            modulation(0)
            dve.tensor_copy(bv_cols, bias_t[:, BV:BV + KC].unsqueeze(2).to_broadcast([P, KC, P])).then_inc(bv_spread, 1)
            for t in range(CT):
                if t % (CT // 2) == 0:
                    dve.wait_ge(c_pool, 4 * t // CT + 2)
                dve.tensor_scalar(cx[:, t, :], cx[:, t, :], cmv[:, t, 0:1], crstd[:, t:t + 1],
                                  ALU.subtract, ALU.mult).then_inc(cx_ready, 1)
            def limits():
                dve.wait_ge(mod_ready, 4)
                for at, src in ((2, one_sc[:].rearrange("p b k -> p (b k)")), (3, sc_kv[:].rearrange("p k b -> p (k b)")),
                                (4, sh_q[:].rearrange("p k b -> p (k b)")), (5, sh_kv[:].rearrange("p k b -> p (k b)")),
                                (6, bias_t[:, BQ:BQ + KC]), (7, bias_t[:, BK:BK + KC])):
                    dve.tensor_reduce(lim[:, at:at + 1], src, AX_X, ALU.max, apply_absolute_value=True)\
                       .then_inc(lim_done, 1)

            def scales():
                dve.wait_ge(lim_red, 2)
                dve.tensor_tensor(lim_sum[:, :], lim_all[:, 2:4], lim_all[:, 4:6], ALU.add).then_inc(lim_step, 1)
                dve.wait_ge(lim_step, 1)
                dve.tensor_tensor(lim_sum[:, :], lim_sum[:, :], lim_f[:, :], ALU.mult).then_inc(lim_step, 1)
                dve.wait_ge(lim_step, 2)
                dve.scalar_tensor_tensor(out=lim_sum[:, :], in0=lim_sum[:, :], scalar=float((H * P) ** 0.5),
                                         in1=lim_all[:, 6:8], op0=ALU.mult, op1=ALU.add).then_inc(lim_step, 1)
                dve.wait_ge(lim_step, 3)
                dve.tensor_scalar(lim_sum[:, :], lim_sum[:, :], 1e-12, 1.0 / TOP, ALU.max, ALU.mult)\
                   .then_inc(lim_step, 1)
                dve.wait_ge(lim_step, 4)
                dve.reciprocal(lim_sum[:, :], lim_sum[:, :]).then_inc(lim_step, 1)
                dve.wait_ge(lim_step, 5)
                dve.tensor_scalar(qk_scale[:, :].bitcast(U32), lim_sum[:, :].bitcast(U32), EXPONENT_BITS, None,
                                  ALU.bitwise_and).then_inc(lim_step, 1)
                dve.wait_ge(lim_step, 6)
                dve.tensor_scalar(one_sc[:, :, :], one_sc[:, :, :], qk_scale[:, 0:1], None, ALU.mult)\
                   .then_inc(lim_step, 1)
                dve.tensor_tensor(exp_scale[:, :], qk_scale[:, 0:1], qk_scale[:, 1:2], ALU.mult).then_inc(lim_step, 1)
                dve.wait_ge(lim_step, 8)
                dve.reciprocal(exp_scale[:, :], exp_scale[:, :]).then_inc(lim_step, 1)
                dve.wait_ge(lim_step, 9)
                dve.tensor_scalar(exp_scale[:, :], exp_scale[:, :], DH ** -0.5, None, ALU.mult).then_inc(lim_step, 1)

            def keys(n):
                m = n % KC
                dve.wait_ge(k_mm, n + 1)
                wait(dve, k_ready, n - 1)
                dve.tensor_scalar(k32[n % 2], ps_v[:, n % 2, :], bias_t[:, BK + m:BK + m + 1], qk_scale[:, 1:2],
                                  ALU.add, ALU.mult).then_inc(k32_done, 1)

            def value_max(t):
                dve.wait_ge(v_copied, t + 1)
                dve.tensor_reduce(v_inv[:, t, :], row_slots[:, t % 2, :].rearrange("p (h d) -> p h d", d=DH),
                                  AX_X, ALU.max, apply_absolute_value=True).then_inc(v_max, 1)

            def value_power(t):
                dve.wait_ge(v_red, t + 1)
                dve.tensor_scalar(v_scale[:, t, :], v_scale[:, t, :], 1e-30, 1.0 / TOP, ALU.max, ALU.mult)\
                   .then_inc(v_step, 1)
                dve.wait_ge(v_step, 3 * t + 1)
                dve.tensor_scalar(v_scale[:, t, :].bitcast(U32), v_scale[:, t, :].bitcast(U32), EXPONENT_BITS, None,
                                  ALU.bitwise_and).then_inc(v_step, 1)
                dve.wait_ge(v_step, 3 * t + 2)
                dve.reciprocal(v_inv[:, t, :], v_scale[:, t, :]).then_inc(v_step, 1)

            def value_place(t):
                s = t % 2
                dve.wait_ge(v_hi_done, t + 1)
                dve.tensor_tensor(v16[1][:, s, :], row_slots[:, s, :], v16[0][:, s, :], ALU.subtract)\
                   .then_inc(v_lo_done, 1)
                dve.wait_ge(v_lo_done, t + 1)
                place(dve.tensor_copy, 1, t).then_inc(v_placed, 1)

            def stats(b, off):
                if exists(b, off):
                    wait(dve, ln_mv, unit(b, off))
                    wait(dve, x_loaded[off % 4], 16 * (2 * b + off // 4 + 1))
                    dve.bn_stats(st[:, :], x_in[:, off % 4, :]).then_inc(ln_bn, 1)

            def await_stats(b, off):
                if exists(b, off):
                    wait(dve, xh_ready, unit(b, off - 1))
                    wait(dve, ln_bn, upto(b, off))

            def mean_var(b, off):
                if exists(b, off):
                    dve.bn_aggr(mv[:, off % 2, :], st[:, :]).then_inc(ln_mv, 1)

            def turned_x(b, off):
                if not exists(b, off):
                    return
                s = (off // 4) % 2
                cols = slice(P * (off % 4), P * (off % 4 + 1))
                wait(dve, xT_hi_done, upto(b, off))
                dve.tensor_tensor(xT_lo[:, s, :, cols], ps_t[:, 0, :].rearrange("p (k n) -> p k n", k=KC),
                                  xT_hi[:, s, :, cols].bitcast(F32), ALU.subtract).then_inc(xT_done, 1)

            def turned_o(b, off):
                if not exists(b, off):
                    return
                wait(dve, oT_hi_done, upto(b, off))
                dve.tensor_tensor(oT_lo[:, :, :], ps_t[:, bank_o(b, off), :].rearrange("p (k n) -> p k n", k=KC),
                                  oT_hi[:].bitcast(F32), ALU.subtract).then_inc(oT_done, 1)

            def denominators(b, off):
                if exists(b, off):
                    for h in range(2):
                        wait(dve, pv_mm, 2 * unit(b, off) + h + 1)
                        dve.reciprocal(rden[:, HALF * h:HALF * (h + 1)], ps_v[:, h, DH:HALF * VC:VC])\
                           .then_inc(rden_done, 1)

            def weights_o(b, off):
                if exists(b, off):
                    wait(dve, o_done, 2 * unit(b, off))
                    wait(dve, rden_done, 2 * upto(b, off))
                    dve.tensor_tensor(rscale[:, :], rden[:, :], cur_vs[:, :], ALU.mult).then_inc(rscale_done, 1)

            def normalise_o(b, off):
                if not exists(b, off):
                    return
                wait(dve, rscale_done, upto(b, off))
                wait(dve, o_turned, unit(b, off))
                for h in range(2):
                    hs = slice(HALF * h, HALF * (h + 1))
                    dve.tensor_tensor(o[:, hs, :],
                                      ps_v[:, h, 0:HALF * VC].rearrange("p (h c) -> p h c", c=VC)[:, :, 0:DH],
                                      rscale[:, hs].unsqueeze(2).to_broadcast([P, HALF, DH]), ALU.mult)\
                       .then_inc(o_done, 1)

            def key_blocks(b):
                if not batch_exists(b):
                    return
                wait(dve, s_mm, 2 * PER * b)
                for r in range(1, HPG):
                    rows = slice(DH * r, DH * (r + 1))
                    dve.tensor_copy(kb[rows, :, r // 2::2, r % 2, :], k16[rows, b, :, :, :]).then_inc(kb_dve_done, 1)

            def score_max(b, off, h):
                if exists(b, off):
                    wait(dve, s_mm, 2 * unit(b, off) + h + 1)
                    wait(dve, sub_done, 2 * unit(b, off))
                    dve.tensor_reduce(mx[:, HALF * h:HALF * (h + 1)],
                                      ps_s[:, h, :].rearrange("p (h l) -> p h l", l=LKV), AX_X, ALU.max)\
                       .then_inc(mx_done, 1)

            def softmax_shift(b, off):
                if not exists(b, off):
                    return
                wait(dve, p_turned, 2 * unit(b, off - 1))
                for h in range(2):
                    hs = slice(HALF * h, HALF * (h + 1))
                    wait(dve, mx_done, 2 * unit(b, off) + h + 1)
                    dve.tensor_tensor(pr[:, off % 2, hs, :], ps_s[:, h, :].rearrange("p (h l) -> p h l", l=LKV),
                                      mx[:, hs].unsqueeze(2).to_broadcast([P, HALF, LKV]), ALU.subtract)\
                       .then_inc(sub_done, 1)

            def turned_p(b, off, h):
                if not exists(b, off):
                    return
                wait(dve, pt_hi_done, 2 * unit(b, off) + h + 1)
                dve.tensor_tensor(pt_lo[:, 4 * h:4 * h + 4, :], ps_t[:, h, :].rearrange("p (g n) -> p g n", g=4),
                                  pt_hi[:, 4 * h:4 * h + 4, :], ALU.subtract).then_inc(pt_done, 1)

            def query(b, off, bank=ps_q):
                if not exists(b, off):
                    return
                s, m = (off // 4) % 2, off % 4
                wait(dve, q_hi_done, 2 * upto(b, off))
                for pair in range(2):
                    rows, to = slice(64 * pair, 64 * (pair + 1)), slice(64 * (1 - pair), 64 * (2 - pair))
                    dve.scalar_tensor_tensor(out=qs[to, s, 2 * m + pair, :], in0=bank[rows, :],
                                             scalar=cur_bq[rows, m:m + 1], in1=qs[rows, s, 2 * m + pair, :],
                                             op0=ALU.add, op1=ALU.subtract).then_inc(q_done, 1)

            def step(b, i):
                if not (isinstance(b, int) and b == 0 and i == 0):
                    turned_x(b, i + 7)
                stats(b, i + 8)
                await_stats(b, i + 8)
                turned_o(b, i - 3)
                mean_var(b, i + 8)
                if i == 2 and batch_exists(b):
                    wait(dve, rscale_done, unit(b, 0))
                    dve.tensor_copy(cur_vs[:, :], v_scale_b[:, b, :]).then_inc(vs_staged, 1)
                denominators(b, i - 2)
                score_max(b, i, 0)
                if i == 2 and batch_exists(b):
                    wait(dve, vs_staged, b + 1)
                weights_o(b, i - 2)
                score_max(b, i, 1)
                normalise_o(b, i - 2)
                softmax_shift(b, i)
                if i == 7:
                    key_blocks(b + 1)
                turned_p(b, i - 1, 0)
                turned_p(b, i - 1, 1)
                query(b, i + 4)

            def output_bias():
                dve.wait_ge(bv_mm, 1)
                dve.wait_ge(ld_bp, 16)
                dve.tensor_tensor(bp_row[:, :], ps_o[:, :], bp_row[:, :], ALU.add).then_inc(bias_ready, 1)

            def prime():
                def first_wq_lo(m):
                    dve.wait_ge(w_hi_done, m + 1)
                    cols = slice(P * m, P * (m + 1))
                    dve.tensor_tensor(w_lo[:, :, cols], w_tmp[:, :, :], w_hi[:, :, cols].bitcast(F32), ALU.subtract)\
                       .then_inc(w_done, 1)

                def all_stats(f):
                    stats(0, f)
                    await_stats(0, f)
                    mean_var(0, f)

                for n in range(2 * KC):
                    half, k = n // KC, n % KC
                    seg = turned[n % TURNED].rearrange("p (b l) -> p b l", b=BH)
                    sc = sc_kv[:, k, BH * half:BH * (half + 1)].unsqueeze(2).to_broadcast([P, BH, LKV])
                    sh = sh_kv[:, k, BH * half:BH * (half + 1)].unsqueeze(2).to_broadcast([P, BH, LKV])
                    if n == 0:
                        modulation(1)
                        dve.wait_ge(mod_ready, 2)
                    dve.wait_ge(cx_turned, n + 1)
                    wait(dve, cT_done, n - TURNED + 1)
                    dve.tensor_tensor(seg, ps_t[:, n % 2, :].rearrange("p (b l) -> p b l", b=BH), sc, ALU.mult)\
                       .then_inc(c_mul, 1)
                    dve.wait_ge(c_mul, n + 1)
                    dve.tensor_tensor(seg, seg, sh, ALU.add).then_inc(c_mod, 1)
                    if n == 1:
                        limits()
                        dve.wait_ge(wv_hi_done, 1)
                        dve.tensor_tensor(wv_lo, wv_raw, wv_hi.bitcast(F32), ALU.subtract).then_inc(wv_done, 1)
                    if n > KC + 1:
                        first_wq_lo(n - KC - 2)
                    if n == KC + 1:
                        scales()
                    if n == KC:
                        dve.wait_ge(wk_hi_done, 1)
                        dve.tensor_tensor(wk_lo, wk_raw, wk_hi.bitcast(F32), ALU.subtract).then_inc(wk_done, 1)

                dve.wait_ge(bq_mm, KC)
                dve.tensor_tensor(bqT[:].rearrange("p b m -> p m b"),
                                  ps_q[:, 0:KC * B].rearrange("p (m b) -> p m b", b=B),
                                  bias_t[:, BQ:BQ + KC].unsqueeze(2).to_broadcast([P, KC, B]), ALU.add)\
                   .then_inc(bq_ready, 1)
                dve.wait_ge(bq_ready, 1)
                dve.tensor_scalar(bqT[:, :, :], bqT[:, :, :], qk_scale[:, 0:1], None, ALU.mult).then_inc(bq_ready, 1)

                for t in range(CT + 1):
                    if 0 < t < CT:
                        keys(t - 1)
                    if t < CT:
                        value_max(t)
                    if t == 6:
                        first_wq_lo(KC - 2)
                    if t == CT - 1:
                        turned_x(0, KC)
                    if t == CT:
                        query(0, 2, first_banks[0])
                        turned_x(0, KC + 2)
                        query(0, 3, first_banks[1])
                        turned_x(0, KC + 3)
                    if t == CT:
                        keys(CT - 1)
                    if t < CT:
                        value_power(t)
                        all_stats(t)
                    if t == 3:
                        output_bias()
                    if t > 0:
                        value_place(t - 1)
                    if 2 <= t <= KC + 1:
                        turned_x(0, t - 2)
                    if t == KC + 1:
                        dve.wait_ge(k_ready, KC)
                        dve.wait_ge(bd_ready, 3)
                        key_blocks(0)
                    if CT - 2 <= t < CT:
                        query(0, t - CT + 2, first_banks[t % 2])
                    if t == CT - 1:
                        turned_x(0, KC + 1)
                        first_wq_lo(KC - 1)
                dve.tensor_copy(v_scale_b[:].rearrange("p (t e) h -> p t e h", e=2),
                                v_scale[:].unsqueeze(2).to_broadcast([P, CT, 2, NH])).then_inc(vs_spread, 1)
                dve.wait_ge(vs_spread, 1)

            every_step(dve, step, prime)

        @block.tensor
        def _(pe):
            pe.wait_ge(id_ready, 1)
            pe.wait_ge(ld_small, 16 * 5)
            pe.transpose(ps_t[:, 0, 0:7 * KC], brow, ident[0:7 * KC, 0:7 * KC]).then_inc(small_turned, 1)
            for k in range(KC):
                last = pe.transpose(ps_t[:, 1, B * k:B * (k + 1)], c_row[:, P * k:P * (k + 1)], ident[0:B, 0:B])
            last.then_inc(small_turned, 1)

            pe.wait_ge(silu_step, 3)
            def modulate(side, landed):
                for k in range(KC):
                    pe.wait_ge(landed[k], 16)
                    for a in range(2):
                        last = pe.matmul((ps_s, ps_v)[side][0:B, a, :], silu_t[:, k, :],
                                         wss[side][:, k, H * a:H * (a + 1)], start=(k == 0), stop=(k == KC - 1))
                last.then_inc(mod_mm, 1)

            def turn_modulation(side):
                pe.wait_ge(mod_copied, side + 1)
                for m in range(2 * KC):
                    last = pe.transpose(ps_t[:, side, B * m:B * (m + 1)], mod_rows[side][:, P * m:P * (m + 1)],
                                        ident[0:B, 0:B])
                last.then_inc(mod_turned, 1)

            def turn_context(n):
                half, k = n // KC, n % KC
                wait(pe, c_mul, n - 1)
                for t in range(4):
                    pe.wait_ge(cx_ready, 4 * half + t + 1)
                    last = pe.transpose(ps_t[:, n % 2, P * t:P * (t + 1)], cx[:, 4 * half + t, P * k:P * (k + 1)],
                                        ident[:, :])
                last.then_inc(cx_turned, 1)

            def shift_product(m):
                for k in range(KC):
                    last = pe.matmul(ps_q[:, B * m:B * (m + 1)], wq[:, k, P * m:P * (m + 1)], sh_q[:, k, :],
                                     start=(k == 0), stop=(k == KC - 1))
                last.then_inc(bq_mm, 1)

            modulate(0, ld_ss)
            turn_modulation(0)
            modulate(1, ld_ssq)
            pe.wait_ge(mod_ready, 2)
            turn_context(0)
            turn_modulation(1)
            pe.wait_ge(mod_ready, 4)
            for m in range(KC):
                turn_context(m + 1)
                if m == 0:
                    pe.wait_ge(ld_wq, 16)
                shift_product(m)
            turn_context(5)

            def split_product(dst, terms):
                last = None
                for n, (a, b) in enumerate((terms(p, k) for p in ((0, 0), (0, 1), (1, 0)) for k in range(KC))):
                    last = pe.matmul(dst, a, b, start=(n == 0), stop=(n == 3 * KC - 1))
                return last

            def value_rows(t):
                wait(pe, v_copied, t - 1)
                half, cols = t // 4, slice(P * (t % 4), P * (t % 4 + 1))
                split_product(ps_s[:, t % 2, :], lambda p, k: (
                    (cT_hi, cT_lo)[p[0]][half][:, k, cols], (wv_hi, wv_lo)[p[1]][:, k, :])).then_inc(v_mm, 1)

            def key_rows(n):
                half, m = n // KC, n % KC
                wait(pe, k32_done, n - 1)
                split_product(ps_v[:, n % 2, :], lambda p, k: (
                    (wk_hi, wk_lo)[p[0]][:, k, P * m:P * (m + 1)],
                    (cT_hi, cT_lo)[p[1]][half][:, k, :])).then_inc(k_mm, 1)

            def bias_product():
                pe.wait_ge(bv_spread, 1)
                pe.wait_ge(ld_wp, 16)
                for k in range(KC):
                    last = pe.matmul(ps_o[:, :], bv_cols[:, k, :], wp_raw[:, k, :], start=(k == 0), stop=(k == KC - 1))
                last.then_inc(bv_mm, 1)

            def turn_x(b, off):
                if not exists(b, off):
                    return
                wait(pe, xh_ready, upto(b, off))
                wait(pe, xT_done, unit(b, off))
                wait(pe, pt_done, 2 * unit(b, off - 9) + 1)
                for k in range(KC):
                    last = pe.transpose(ps_t[:, 0, P * k:P * (k + 1)], xh[:, off % 2, P * k:P * (k + 1)], ident[:, :])
                last.then_inc(xT_turned, 1)

            def project(b, off, bank=ps_q, spare=0):
                if not exists(b, off):
                    return
                s, m = (off // 4) % 2, off % 4
                if m == 0:
                    wait(pe, xT_done, upto(b, off + 3))
                if off % PER < 4:
                    wait(pe, w_done, KC * (b + off // PER) + m + 1)
                wait(pe, q_done, 2 * (unit(b, off) - spare))
                cols = slice(P * m, P * (m + 1))
                n = 0
                for w, xt in ((w_hi, xT_hi), (w_hi, xT_lo), (w_lo, xT_hi)):
                    for k in range(KC):
                        last = pe.matmul(bank[:, :], w[:, k, cols], xt[:, s, k, :], start=(n == 0),
                                         stop=(n == 3 * KC - 1))
                        n += 1
                last.then_inc(q_mm, 1)

            def score(b, off):
                if not exists(b, off):
                    return
                s = (off // 4) % 2
                cols = slice(P * (off % 4), P * (off % 4 + 1))
                if off % 4 == 0:
                    wait(pe, q_done, 2 * upto(b, off + 3))
                if off % PER == 0:
                    wait(pe, kb_dve_done, 3 * (b + 1))
                    wait(pe, kb_act_done, 5 * (b + 1))
                for h in range(2):
                    wait(pe, sub_done, 2 * unit(b, off - 1) + h + 1)
                    for g in range(4):
                        pair = 4 * h + g
                        for part in range(2):
                            last = pe.matmul(ps_s[:, h, P * g:P * (g + 1)], qs[:, s, pair, cols],
                                             kb[:, part, pair, :, :].rearrange("p h l -> p (h l)"),
                                             start=(part == 0), stop=(part == 1))
                    last.then_inc(s_mm, 1)

            def turn_p(b, off):
                if not exists(b, off):
                    return
                wait(pe, exp_done, upto(b, off))
                for h in range(2):
                    if h == 0:
                        wait(pe, xT_done, upto(b, off + 8))
                    if bank_o(b, off - 2) == h:
                        wait(pe, oT_done, unit(b, off - 1))
                    wait(pe, pt_done, 2 * unit(b, off - 1) + h + 1)
                    for g in range(4):
                        pair = 4 * h + g
                        last = pe.transpose(ps_t[:, h, P * g:P * (g + 1)],
                                            pr[:, off % 2, 2 * pair:2 * pair + 2, :].rearrange("p h l -> p (h l)"),
                                            ident[:, :])
                    last.then_inc(p_turned, 1)

            def weigh(b, off):
                if not exists(b, off):
                    return
                if off % PER == 0:
                    wait(pe, vb_done, 4 * (b + off // PER + 1))
                wait(pe, o_done, 2 * unit(b, off))
                for h in range(2):
                    wait(pe, pt_done, 2 * unit(b, off) + h + 1)
                    for g in range(4):
                        pair = 4 * h + g
                        dst = ps_v[:, h, 2 * VC * g:2 * VC * (g + 1)]
                        for n, (pt, part) in enumerate(((pt_hi, 0), (pt_hi, 1), (pt_lo, 0))):
                            last = pe.matmul(dst, pt[:, pair, :],
                                             vb[:, part, pair, :, :].rearrange("p h c -> p (h c)"),
                                             start=(n == 0), stop=(n == 2))
                    last.then_inc(pv_mm, 1)

            def turn_o(b, off):
                if not exists(b, off):
                    return
                wait(pe, o_done, 2 * upto(b, off))
                wait(pe, oT_done, unit(b, off))
                wait(pe, pt_done, 2 * unit(b, off + 1) + bank_o(b, off) + 1 if exists(b, off + 1) else 2 * UNITS)
                for k in range(KC):
                    last = pe.transpose(ps_t[:, bank_o(b, off), P * k:P * (k + 1)],
                                        o[:, HPG * k:HPG * (k + 1), :].rearrange("p h d -> p (h d)"), ident[:, :])
                last.then_inc(o_turned, 1)

            def project_out(b, off):
                if not exists(b, off):
                    return
                if isinstance(b, int) and b == 0:
                    wait(pe, wp_ready, 2)
                wait(pe, oT_done, upto(b, off))
                wait(pe, y_copied, unit(b, off))
                n = 0
                for ot, w in ((oT_hi, wp_hi), (oT_hi, wp_lo), (oT_lo, wp_hi)):
                    for k in range(KC):
                        last = pe.matmul(ps_o[:, :], ot[:, k, :], w[:, k, :], start=(n == 0), stop=(n == 3 * KC - 1))
                        n += 1
                last.then_inc(out_mm, 1)

            def step(b, i):
                score(b, i)
                project(b, i + 4)
                turn_p(b, i - 1)
                project_out(b, i - 3)
                turn_x(b, i + 8)
                turn_o(b, i - 2)
                weigh(b, i - 1)

            def prime():
                pe.wait_ge(cT_done, KC)
                pe.wait_ge(wv_done, 1)
                value_rows(0)
                turn_context(6)
                turn_context(7)
                pe.wait_ge(wk_done, 1)
                key_rows(0)
                for n in range(1, CT):
                    if n == KC:
                        pe.wait_ge(cT_done, 2 * KC)
                    value_rows(n)
                    if n == CT - 1:
                        turn_x(0, KC)
                    if n < CT - 1:
                        key_rows(n)
                    if n == 1:
                        bias_product()
                    if 2 <= n <= KC + 1:
                        turn_x(0, n - 2)
                    if n == KC + 2:
                        pe.wait_ge(bq_ready, 1)
                        pe.wait_ge(bias_ready, 1)
                        project(0, 0, first_banks[0], 1)
                for m in range(1, KC):
                    project(0, m, first_banks[m % 2], 1)
                    turn_x(0, KC + m)
                key_rows(CT - 1)

            every_step(pe, step, prime)


_INS = ["x", "ctx_1024", "cond_1024", "L0_xcond_Wq", "L0_xcond_bq", "L0_xcond_Wkv", "L0_xcond_bkv", "L0_xcond_Wp",
        "L0_xcond_bp", "L0_xcond_Wss_q", "L0_xcond_bss_q", "L0_xcond_Wss_kv", "L0_xcond_bss_kv"]
_OUTS = [((16, 1024, 512), "float32")]


def kernel(**inputs):
    import numpy as _np
    import concourse.bacc as _bacc
    from concourse import mybir as _mybir
    from concourse.bass_utils import run_bass_kernel_spmd as _run

    nc = _bacc.Bacc("TRN2", target_bir_lowering=False, num_devices=1)
    arrays, args = {}, []
    for name in _INS:
        a = _np.ascontiguousarray(inputs[name])
        arrays[f"in_{name}_dram"] = a
        args.append(nc.dram_tensor(f"in_{name}_dram", a.shape, _mybir.dt.from_np(a.dtype), kind="ExternalInput").ap())
    for i, (shape, dtype) in enumerate(_OUTS):
        dt = _mybir.dt.from_np(_np.dtype(dtype))
        args.append(nc.dram_tensor(f"out_{i}_dram", shape, dt, kind="ExternalOutput").ap())
    adaln_cross_attention(nc, *args)
    r = _run(nc, [arrays], core_ids=[0])
    return r.results[0]["out_0_dram"]
```
